# Optimizing a Trainium2 kernel written in Bass

```python
import numpy as np
import jax
import jax.numpy as jnp

def _softmax(x, axis=-1):
    return jax.nn.softmax(x, axis=axis)
def _gelu(x):
    return jax.nn.gelu(x, approximate=True)
def _silu(x):
    return jax.nn.silu(x)
def _sigmoid(x):
    return jax.nn.sigmoid(x)
def _layernorm(x, axis=-1, eps=1e-5):
    m = jnp.mean(x, axis=axis, keepdims=True)
    v = jnp.var(x, axis=axis, keepdims=True)
    return (x - m) / jnp.sqrt(v + eps)
def _scatter_add(tgt, idx, src, axis=0):
    return tgt.at[idx].add(src)
def _segment_sum(src, seg, n):
    return jax.ops.segment_sum(src, seg, n)

kernel_name = 'mk_adj_resnorm_d4_adj_128_40b2a5'

def setup_inputs(seed: int = 0):
    np.random.seed(seed)
    _w = jnp.asarray
    def _rec_inputs():
        import jax
        import jax.numpy as jnp
        _gk = jax.random.key(seed)
        x = -0.0002928 + 1 * jax.random.normal(jax.random.fold_in(_gk, 1), (32, 512, 128), jnp.float32)
        _w = (1.0 + jnp.arange(512, dtype=jnp.float32)) ** -0.5
        _w = _w / _w.mean()
        _pij = jnp.clip(0.0078125 * _w[:, None] * _w[None, :], 0.0, 1.0)
        _a = jax.random.uniform(jax.random.fold_in(_gk, 2), (512, 512)) < _pij
        _a = jnp.logical_or(_a, jnp.swapaxes(_a, -1, -2))
        _a = jnp.logical_or(_a, jnp.eye(512, dtype=bool))
        _af = _a.astype(jnp.float32)
        _af = _af * jax.random.uniform(jax.random.fold_in(_gk, 3), (512, 512), jnp.float32, 0.05, 1)
        adj = _af
        return x, adj
    x, adj = _rec_inputs()
    def _L0_gnn_setup():
        import jax, jax.numpy as jnp
        import numpy as np
        B, N, D = (32, 1024, 128)
        TIME_STEP = 5
        key = jax.random.key(seed)
        ks = jax.random.split(key, 12)
        s2 = 1.0 / np.sqrt(2 * D)
        s1 = 1.0 / np.sqrt(D)
        return {'input': jax.random.normal(ks[0], (B, N, D), jnp.float32), 'in_matrix': jax.random.uniform(ks[1], (N, N), jnp.float32), 'out_matrix': jax.random.uniform(ks[2], (N, N), jnp.float32), 'w3_w': jax.random.normal(ks[3], (D, 2 * D), jnp.float32) * s2, 'w3_b': jnp.zeros((D,), jnp.float32), 'u3_w': jax.random.normal(ks[4], (D, D), jnp.float32) * s1, 'u3_b': jnp.zeros((D,), jnp.float32), 'w4_w': jax.random.normal(ks[5], (D, 2 * D), jnp.float32) * s2, 'w4_b': jnp.zeros((D,), jnp.float32), 'w5_w': jax.random.normal(ks[6], (D, 2 * D), jnp.float32) * s2, 'w5_b': jnp.zeros((D,), jnp.float32), 'u5_w': jax.random.normal(ks[7], (D, D), jnp.float32) * s1, 'u5_b': jnp.zeros((D,), jnp.float32), 'time_step': TIME_STEP}
    _L0_gnn_all = _L0_gnn_setup()
    _L0_gnn_in = {k: v for k, v in _L0_gnn_all.items() if k in ('w3_w', 'w3_b', 'u3_w', 'u3_b', 'w4_w', 'w4_b', 'w5_w', 'w5_b', 'u5_w', 'u5_b', )}
    del _L0_gnn_all

    def _L1_gnn_setup():
        import jax, jax.numpy as jnp
        import numpy as np
        B, N, D, OUT = (8, 2048, 128, 128)
        key = jax.random.key(seed)
        k1, k2, k3, k4, k5, k6 = jax.random.split(key, 6)
        stdv = 1.0 / np.sqrt(OUT)
        inputs = jax.random.normal(k1, (B, N, D), dtype=jnp.float32)
        relation = jax.random.normal(k2, (N, N), dtype=jnp.float32)
        gl = 1.0 / np.sqrt(2 * D + 1)
        g_w = jax.random.uniform(k3, (2 * D + 1,), minval=-gl, maxval=gl, dtype=jnp.float32)
        g_b = jax.random.uniform(k4, (), minval=-gl, maxval=gl, dtype=jnp.float32)
        weight = jax.random.uniform(k5, (D, OUT), minval=-stdv, maxval=stdv, dtype=jnp.float32)
        bias = jax.random.uniform(k6, (OUT,), minval=-stdv, maxval=stdv, dtype=jnp.float32)
        return {'inputs': inputs, 'relation': relation, 'g_w': g_w, 'g_b': g_b, 'weight': weight, 'bias': bias}
    _L1_gnn_all = _L1_gnn_setup()
    _L1_gnn_in = {k: v for k, v in _L1_gnn_all.items() if k in ('g_w', 'g_b', 'weight', 'bias', )}
    del _L1_gnn_all

    def _L2_gnn_setup():
        import jax, jax.numpy as jnp
        import numpy as np
        from jax import lax
        CONV_ORDER = 3

        def _chebyshev(adj, x, order):

            def step(carry, _):
                nxt = jnp.einsum('ij,bjc->bic', adj, carry)
                return (nxt, nxt)
            _, xs = lax.scan(step, x, None, length=order)
            return jnp.moveaxis(xs, 0, -1)
        key = jax.random.key(seed)
        k1, k2, k3, k4 = jax.random.split(key, 4)
        B, E, C_in, C_out, K, n_adjs = (8, 4096, 128, 128, CONV_ORDER, 2)
        x_1 = jax.random.normal(k1, (B, E, C_in), dtype=jnp.float32)
        adj0 = jax.random.normal(k2, (E, E), dtype=jnp.float32) / np.sqrt(E)
        adj1 = jax.random.normal(k3, (E, E), dtype=jnp.float32) / np.sqrt(E)
        kdim = K * n_adjs + 1
        std = 1.414 * np.sqrt(2.0 / float((C_in + C_out) * kdim))
        weight_1 = std * jax.random.normal(k4, (C_in, C_out, kdim), dtype=jnp.float32)
        return {'x_1': x_1, 'adj0': adj0, 'adj1': adj1, 'weight_1': weight_1}
    _L2_gnn_all = _L2_gnn_setup()
    _L2_gnn_in = {k: v for k, v in _L2_gnn_all.items() if k in ('weight_1', )}
    del _L2_gnn_all

    def _L3_gnn_setup():
        import jax, jax.numpy as jnp
        import numpy as np
        B, N, F_IN, F_OUT = (8, 2048, 128, 128)
        ALPHA = 0.1
        NEG_BIG = -9000000000000000.0

        def _pair_indices(n):
            m = jnp.arange(n)[:, None] * n + jnp.arange(n)[None, :]
            nn = n * n
            k1, k2 = (2 * m, 2 * m + 1)
            idx1 = jnp.where(k1 < nn, k1 // n, k1 % n)
            idx2 = jnp.where(k2 < nn, k2 // n, k2 % n)
            return (idx1, idx2)
        key = jax.random.key(seed)
        k1, k2, k3, k4 = jax.random.split(key, 4)
        x = jax.random.normal(k1, (B, N, F_IN), dtype=jnp.float32)
        adj = jnp.ones((N, N), dtype=jnp.float32) - jnp.eye(N, dtype=jnp.float32)
        others_weight = jax.random.normal(k2, (F_IN, F_OUT), dtype=jnp.float32) * (1.0 / np.sqrt(F_OUT))
        self_weight = jax.random.normal(k3, (F_IN, F_OUT), dtype=jnp.float32) * (1.0 / np.sqrt(F_OUT))
        att_weight = jax.random.normal(k4, (2 * F_OUT, 1), dtype=jnp.float32)
        return {'x': x, 'adj': adj, 'others_weight': others_weight, 'self_weight': self_weight, 'att_weight': att_weight}
    _L3_gnn_all = _L3_gnn_setup()
    _L3_gnn_in = {k: v for k, v in _L3_gnn_all.items() if k in ('others_weight', 'self_weight', 'att_weight', )}
    del _L3_gnn_all

    return {
        "x": x,
        "adj": adj,
        "L0_gnn_w3_w": _L0_gnn_in["w3_w"],
        "L0_gnn_w3_b": _L0_gnn_in["w3_b"],
        "L0_gnn_u3_w": _L0_gnn_in["u3_w"],
        "L0_gnn_u3_b": _L0_gnn_in["u3_b"],
        "L0_gnn_w4_w": _L0_gnn_in["w4_w"],
        "L0_gnn_w4_b": _L0_gnn_in["w4_b"],
        "L0_gnn_w5_w": _L0_gnn_in["w5_w"],
        "L0_gnn_w5_b": _L0_gnn_in["w5_b"],
        "L0_gnn_u5_w": _L0_gnn_in["u5_w"],
        "L0_gnn_u5_b": _L0_gnn_in["u5_b"],
        "L1_gnn_g_w": _L1_gnn_in["g_w"],
        "L1_gnn_g_b": _L1_gnn_in["g_b"],
        "L1_gnn_weight": _L1_gnn_in["weight"],
        "L1_gnn_bias": _L1_gnn_in["bias"],
        "L2_gnn_weight_1": _L2_gnn_in["weight_1"],
        "L3_gnn_others_weight": _L3_gnn_in["others_weight"],
        "L3_gnn_self_weight": _L3_gnn_in["self_weight"],
        "L3_gnn_att_weight": _L3_gnn_in["att_weight"],
    }

def reference(x, adj, L0_gnn_w3_w, L0_gnn_w3_b, L0_gnn_u3_w, L0_gnn_u3_b, L0_gnn_w4_w, L0_gnn_w4_b, L0_gnn_w5_w, L0_gnn_w5_b, L0_gnn_u5_w, L0_gnn_u5_b, L1_gnn_g_w, L1_gnn_g_b, L1_gnn_weight, L1_gnn_bias, L2_gnn_weight_1, L3_gnn_others_weight, L3_gnn_self_weight, L3_gnn_att_weight):
    import jax
    import jax.numpy as jnp
    def _L0_gnn_ref(input, in_matrix, out_matrix, w3_w, w3_b, u3_w, u3_b, w4_w, w4_b, w5_w, w5_b, u5_w, u5_b, time_step):
        import jax, jax.numpy as jnp
        import numpy as np
        B, N, D = (32, 1024, 128)
        TIME_STEP = 5
        def step(h, _):
            m_in = jnp.einsum('nm,bmd->bnd', in_matrix, h)
            m_out = jnp.einsum('nm,bmd->bnd', out_matrix, h)
            av = jnp.concatenate([m_in, m_out], axis=-1)
            u3 = h @ u3_w.T + u3_b
            z = jax.nn.sigmoid(av @ w3_w.T + w3_b + u3)
            r = jax.nn.sigmoid(av @ w4_w.T + w4_b + u3)
            hv = jnp.tanh(av @ w5_w.T + w5_b + (r * h @ u5_w.T + u5_b))
            h = (1.0 - z) * h + z * hv
            return (h, None)
        h, _ = jax.lax.scan(step, input, None, length=time_step)
        return h

    def _L1_gnn_ref(inputs, relation, g_w, g_b, weight, bias):
        import jax, jax.numpy as jnp
        import numpy as np
        B, N, D, OUT = (8, 2048, 128, 128)
        b, n, d = inputs.shape
        w_j = g_w[:d]
        w_i = g_w[d:2 * d]
        w_r = g_w[2 * d]
        sj = inputs @ w_j
        si = inputs @ w_i
        res = si[:, :, None] + sj[:, None, :] + relation[None] * w_r + g_b
        agg = jnp.einsum('bij,bjd->bid', res, inputs)
        return agg @ weight + bias

    def _L2_gnn_ref(x_1, adj0, adj1, weight_1):
        import jax, jax.numpy as jnp
        import numpy as np
        from jax import lax
        CONV_ORDER = 3

        def _chebyshev(adj, x, order):

            def step(carry, _):
                nxt = jnp.einsum('ij,bjc->bic', adj, carry)
                return (nxt, nxt)
            _, xs = lax.scan(step, x, None, length=order)
            return jnp.moveaxis(xs, 0, -1)
        parts = [x_1[..., None], _chebyshev(adj0, x_1, CONV_ORDER), _chebyshev(adj1, x_1, CONV_ORDER)]
        x_all = jnp.concatenate(parts, axis=3)
        y_1 = jnp.einsum('bnik,iok->bno', x_all, weight_1)
        return y_1

    def _L3_gnn_ref(x, adj, others_weight, self_weight, att_weight):
        import jax, jax.numpy as jnp
        import numpy as np
        B, N, F_IN, F_OUT = (8, 2048, 128, 128)
        ALPHA = 0.1
        NEG_BIG = -9000000000000000.0

        def _pair_indices(n):
            m = jnp.arange(n)[:, None] * n + jnp.arange(n)[None, :]
            nn = n * n
            k1, k2 = (2 * m, 2 * m + 1)
            idx1 = jnp.where(k1 < nn, k1 // n, k1 % n)
            idx2 = jnp.where(k2 < nn, k2 // n, k2 % n)
            return (idx1, idx2)
        b, n, _ = x.shape
        f_out = others_weight.shape[1]
        h = x @ others_weight
        a1 = att_weight[:f_out, 0]
        a2 = att_weight[f_out:, 0]
        u1 = h @ a1
        u2 = h @ a2
        idx1, idx2 = _pair_indices(n)
        e = u1[:, idx1] + u2[:, idx2]
        e = jnp.where(e >= 0, e, ALPHA * e)
        att = jnp.where(adj > 0, e, NEG_BIG)
        att = jax.nn.softmax(att, axis=1)
        out = jnp.einsum('bik,bkl->bil', att, h)
        out = out + x @ self_weight
        return out

    x = _layernorm(x + _L0_gnn_ref(x, adj, adj, L0_gnn_w3_w, L0_gnn_w3_b, L0_gnn_u3_w, L0_gnn_u3_b, L0_gnn_w4_w, L0_gnn_w4_b, L0_gnn_w5_w, L0_gnn_w5_b, L0_gnn_u5_w, L0_gnn_u5_b, 5), axis=-1)
    x = _layernorm(x + _L1_gnn_ref(x, adj, L1_gnn_g_w, L1_gnn_g_b, L1_gnn_weight, L1_gnn_bias), axis=-1)
    x = _layernorm(x + _L2_gnn_ref(x, adj, adj, L2_gnn_weight_1), axis=-1)
    x = _layernorm(x + _L3_gnn_ref(x, adj, L3_gnn_others_weight, L3_gnn_self_weight, L3_gnn_att_weight), axis=-1)
    return x


_drawn_inputs = setup_inputs


def setup_inputs(seed=0):
    import zlib

    import numpy as np

    out = dict(_drawn_inputs(seed))
    spreads = {'L0_gnn_w3_b': (0.0, 0.1),
     'L0_gnn_u3_b': (0.0, 0.1),
     'L0_gnn_w4_b': (0.0, 0.8),
     'L0_gnn_w5_b': (0.0, 0.1),
     'L0_gnn_u5_b': (0.0, 0.1)}
    factors = {'L1_gnn_bias': 8.0}
    for name, (base, spread) in spreads.items():
        noise = np.random.default_rng([zlib.crc32(name.encode()), seed]).standard_normal(out[name].shape)
        drawn = base * np.exp(spread * noise) if base else spread * noise
        out[name] = jnp.asarray(drawn.astype(out[name].dtype))
    for name, factor in factors.items():
        out[name] = (out[name] * factor).astype(out[name].dtype)
    return out
```

```python
from contextlib import ExitStack

import concourse.bass as bass
from concourse import mybir

F32 = mybir.dt.float32
F32R = mybir.dt.float32r
ALU = mybir.AluOpType
ACT = mybir.ActivationFunctionType
AX_X = mybir.AxisListType.X

P = 128
N = 512
NT = N // P
HALF = N // 2
BATCH = 32
SLOTS = 4
GROUPS = BATCH // SLOTS
STEPS = 5
EPS = 1e-5
NEG_BIG = -9000000000000000.0
LEAK = 0.1

(W3A, W3B, W4A, W4B, W5A, W5B, U3, U5, W1, C0, C1, C2, C3, C4, C5, C6, WO, WS, WOT) = range(19)
(B3, B4, B5, BU3, BU5, WJ, BIAS1, A1, A2) = range(9)
(S_R, S_H, S_ZR, S_U3, S_U5, S_W1, S_X0, S_X1, S_X2, S_X3, S_WO, S_WS, S_SJ, S_V, S_P1, S_P2) = range(16)

N_AGG = STEPS + 1 + 3
N_NODES = STEPS + 3
N_SPLIT = STEPS + 3
N_LN = 4
N_CHAN = 3
N_OUT = 3


PRIMED = 1


def gated_count(g, s, b):
    return STEPS * SLOTS * g + SLOTS * s + b + 1


def norm_count(g, k, b):
    norms = [x for x in late_order() if x[0] == "norm"]
    return N_LN * SLOTS * g + norms.index(("norm", k, b)) + 1


def late_order():
    layers = []
    layers += [("norm", 0), ("channels", 0), ("agg", 1), ("sj", 1), ("cols", 1), ("rank1", 1), ("out1", 1), ("turn", 1)]
    layers += [("norm", 1), ("channels", 1), ("agg", 2), ("power", 1), ("power", 2), ("power", 3), ("turn", 2)]
    layers += [("norm", 2), ("channels", 2), ("rows", 3), ("softmax", 3), ("attend", 3), ("turn", 3), ("norm", 3)]
    lag = 1
    order = []
    for t in range(len(layers) + lag * (SLOTS - 1)):
        for b in range(SLOTS):
            if 0 <= t - lag * b < len(layers):
                order.append((*layers[t - lag * b], b))
    return order


def build(nc, x_nodes, x_channels, adj, adj_t, weights, columns, row_in, out):
    with ExitStack() as ctx:
        def sb(name, shape, dt=F32):
            return ctx.enter_context(nc.sbuf_tensor(name, shape, dt))

        def sem(name):
            return ctx.enter_context(nc.semaphore(name))

        def sems(name):
            return [sem(f"{name}{b}") for b in range(SLOTS)]

        ap_hi = [sb(f"adj{k}_hi", [P, NT, N], F32R) for k in (1, 2, 3)]
        ap_lo = [sb(f"adj{k}_lo", [P, NT, N], F32R) for k in (1, 2, 3)]
        w_in = sb("w_in", [P, 19, P])
        w_hi = sb("w_hi", [P, 16, P], F32R)
        w_lo = sb("w_lo", [P, 16, P], F32R)
        cols = sb("cols", [P, 9])
        rows = sb("rows", [1, P + 2])
        wrgb = sb("wrgb", [P, 2])
        ident = sb("ident", [P, P])
        ones = sb("ones", [P, P])
        bias_r = sb("bias_r", [P, 1])
        bias_z = sb("bias_z", [P, 1])
        bias_h = sb("bias_h", [P, 1])
        wo_att = sb("wo_att", [P, 3])
        half_neg = sb("half_neg", [P, NT])
        eps = sb("eps", [P, NT])
        low_neg = sb("low_neg", [P, NT, HALF])
        up_mask = sb("up_mask", [P, NT, HALF], F32R)
        no_up = sb("no_up", [P, NT])
        any_up = sb("any_up", [P, NT])
        up_neg = sb("up_neg", [P, NT])
        up_count = sb("up_count", [P, NT])

        x_in = sb("x_in", [P, SLOTS, N])
        h_ch = sb("h_ch", [P, SLOTS, N])
        chan32 = sb("chan32", [P, SLOTS, N])
        nodes32 = sb("nodes32", [P, SLOTS, N])
        work = sb("work", [P, SLOTS, 2 * N])
        row32 = sb("row32", [P, SLOTS, N])
        nodes_hi_t = sb("nodes_hi_t", [P, SLOTS, N], F32R)
        nodes_lo_t = sb("nodes_lo_t", [P, SLOTS, N], F32R)
        agg_hi_t = sb("agg_hi_t", [P, SLOTS, N], F32R)
        agg_lo_t = sb("agg_lo_t", [P, SLOTS, N], F32R)
        chan_hi_t = sb("chan_hi_t", [P, SLOTS, N], F32R)
        chan_lo_t = sb("chan_lo_t", [P, SLOTS, N], F32R)
        rank_hi_t = sb("rank_hi_t", [P, SLOTS, P], F32R)
        rank_lo_t = sb("rank_lo_t", [P, SLOTS, P], F32R)
        stats_t = sb("stats_t", [P, SLOTS, NT, 6])
        moments_t = sb("moments_t", [P, SLOTS, NT, 2])
        var_t = sb("var_t", [P, SLOTS, NT])
        rstd_t = sb("rstd_t", [P, SLOTS, NT])
        xsum_t = sb("xsum_t", [P, SLOTS, 1])
        tcol_t = sb("tcol_t", [P, SLOTS, 1])
        mix_t = sb("mix_t", [P, SLOTS, 1])
        ccol_t = sb("ccol_t", [P, SLOTS, 1])
        srow_t = sb("srow_t", [1, SLOTS, P])
        trash = sb("trash", [P, N])
        pair_t = sb("pair_t", [P, SLOTS, 2])
        pairl_t = sb("pairl_t", [P, SLOTS, 2])
        lmax_t = sb("lmax_t", [P, SLOTS, NT])
        umax_t = sb("umax_t", [P, SLOTS, NT])
        nmax_t = sb("nmax_t", [P, SLOTS, NT])
        udif_t = sb("udif_t", [P, SLOTS, NT])
        lsum_t = sb("lsum_t", [P, SLOTS, NT])
        uexp_t = sb("uexp_t", [P, SLOTS, NT])
        usum_t = sb("usum_t", [P, SLOTS, NT])
        den_t = sb("den_t", [P, SLOTS, NT])
        rden_t = sb("rden_t", [P, SLOTS, NT])
        uden_t = sb("uden_t", [P, SLOTS, NT])

        bank_a = [ctx.enter_context(nc.psum_tensor(f"bank_a{b}", [P, N], F32)) for b in range(SLOTS)]
        bank_b = [ctx.enter_context(nc.psum_tensor(f"bank_b{b}", [P, N], F32)) for b in range(SLOTS)]

        adj_loaded, adjt_loaded, w_loaded, cols_loaded, rows_loaded = (
            sem(n) for n in ("adj_loaded", "adjt_loaded", "w_loaded", "cols_loaded", "rows_loaded"))
        consts_set, adj_split, w_mixed, w_split, masks_set = (
            sem(n) for n in ("consts_set", "adj_split", "w_mixed", "w_split", "masks_set"))
        prep_small, prep_small_read, power_ready, power_hi, power_lo = (
            sem(n) for n in ("prep_small", "prep_small_read", "power_ready", "power_hi", "power_lo"))
        x_loaded, h_loaded, stored = sems("x_loaded"), sems("h_loaded"), sems("stored")
        agg_ready, agg_hi, agg_lo = sems("agg_ready"), sems("agg_hi"), sems("agg_lo")
        h_done = sems("h_done")
        nodes_ready, nodes_hi, nodes_lo = sems("nodes_ready"), sems("nodes_hi"), sems("nodes_lo")
        normed = sems("normed")
        chan_ready, chan_done, chan_hi, chan_lo = (
            sems(n) for n in ("chan_ready", "chan_done", "chan_hi", "chan_lo"))
        out_ready, resid_done = sems("out_ready"), sems("resid_done")
        rgate_ready, r_done, rh_done = sem("rgate_ready"), sem("r_done"), sem("rh_done")
        zgate_ready, z_done = sem("zgate_ready"), sem("z_done")
        cand_ready, cand_done = sem("cand_ready"), sem("cand_done")
        delta_done, gated_done = sem("delta_done"), sem("gated_done")
        moments_done, var_done, rstd_done = (
            sem(n) for n in ("moments_done", "var_done", "rstd_done"))
        first_sum = sem("first_sum")
        sj_ready, t_done, mix_done = sem("sj_ready"), sem("t_done"), sem("mix_done")
        cols_ready, srow_done, ccol_done = sem("cols_ready"), sem("srow_done"), sem("ccol_done")
        rank_ready, rank_hi, rank_lo = sem("rank_ready"), sem("rank_hi"), sem("rank_lo")
        vrow_ready, vleak_done, vrow_done = sem("vrow_ready"), sem("vleak_done"), sem("vrow_done")
        pair_ready, pair_done, pairl_done = sem("pair_ready"), sem("pair_done"), sem("pairl_done")
        lmax_done, umax_done, lmax2_done, nmax_done, udif_done = (
            sem(n) for n in ("lmax_done", "umax_done", "lmax2_done", "nmax_done", "udif_done"))
        low_done, up_done, usum_done, den_done, rden_done, uden_done = (
            sem(n) for n in ("low_done", "up_done", "usum_done", "den_done", "rden_done", "uden_done"))
        att_ready, hlow_done, hup_done, hup_hi, hup_lo = (
            sem(n) for n in ("att_ready", "hlow_done", "hup_done", "hup_hi", "hup_lo"))

        adj32 = work[:, 0:2, :].rearrange("p s (t n) -> p (s t) n", t=2)
        mixed = work[:, 2:4, :].rearrange("p s (w o) -> p (s w) o", o=P)
        adjt32 = row32
        up32 = nodes32[:, :, 0:HALF]

        block = ctx.enter_context(nc.Block())

        @block.sync
        def _(sp):
            sp.sem_inc(first_sum, PRIMED)
            for b in range(SLOTS):
                sp.sem_inc(nodes_ready[b], PRIMED)
                sp.sem_inc(normed[b], PRIMED)
                sp.sem_inc(stored[b], PRIMED)
            sp.dma_start(adjt32[:, :, :], adj_t.rearrange("(t p) n -> p t n", p=P)).then_inc(adjt_loaded, 16)
            sp.dma_start(adj32, adj.rearrange("(t p) n -> p t n", p=P)).then_inc(adj_loaded, 16)
            with sp.Fori(0, GROUPS) as g:
                for b in range(SLOTS):
                    sp.wait_ge(first_sum, SLOTS * g + PRIMED)
                    sp.dma_start(x_in[:, b, :].rearrange("p (t c) -> p t c", t=NT),
                                 x_nodes[g * SLOTS + b].rearrange("(t p) c -> p t c", p=P)).then_inc(x_loaded[b], 16)
                    sp.wait_ge(nodes_ready[b], N_NODES * g + PRIMED)
                    sp.dma_start(h_ch[:, b, :], x_channels[g * SLOTS + b]).then_inc(h_loaded[b], 16)
                for b in range(SLOTS):
                    sp.wait_ge(normed[b], N_LN * g + N_LN + PRIMED)
                    sp.dma_start(out[g * SLOTS + b].rearrange("(t p) c -> p t c", p=P),
                                 nodes32[:, b, :].rearrange("p (t c) -> p t c", t=NT)).then_inc(stored[b], 16)
            for b in range(SLOTS):
                sp.wait_ge(stored[b], 16 * GROUPS + PRIMED)

        @block.gpsimd
        def _(pool):
            pool.memset(half_neg[:, :], -0.5).then_inc(consts_set, 1)
            pool.memset(ones[:, :], 1.0).then_inc(consts_set, 1)
            pool.memset(ident[:, :], 0.0).then_inc(consts_set, 1)
            pool.memset(eps[:, :], EPS).then_inc(consts_set, 1)
            pool.wait_ge(consts_set, 4)
            pool.affine_select(out=ident[:, :], in_=ident[:, :], compare_op=ALU.not_equal, fill=1.0,
                               base=0, pattern=[[-1, P]], channel_multiplier=1).then_inc(consts_set, 1)

            def rstd(g, k, b):
                pool.wait_ge(moments_done, norm_count(g, k, b))
                pool.tensor_tensor(var_t[:, b, :], moments_t[:, b, :, 1], eps[:, :], ALU.add).then_inc(var_done, 1)
                pool.wait_ge(var_done, norm_count(g, k, b))
                pool.tensor_tensor(rstd_t[:, b, :], var_t[:, b, :], half_neg[:, :], ALU.pow).then_inc(rstd_done, 1)

            with pool.Fori(0, GROUPS) as g:
                for phase, k, b in late_order():
                    if phase == "norm":
                        rstd(g, k, b)

        @block.scalar
        def _(act):
            act.dma_start(w_in[:, :, :], weights).then_inc(w_loaded, 16)
            act.dma_start(cols[:, :], columns).then_inc(cols_loaded, 16)
            act.dma_start(rows[:, :], row_in).then_inc(rows_loaded, 16)
            act.wait_ge(adjt_loaded, 16)
            act.activation(ap_hi[0][:, :, :], adjt32[:, :, :], ACT.Copy).then_inc(adj_split, 1)
            act.wait_ge(adj_loaded, 16)
            act.activation(chan_hi_t[:, :, :], adj32, ACT.Copy).then_inc(adj_split, 1)
            act.wait_ge(w_mixed, 1)
            act.activation(w_hi[:, :, :], mixed, ACT.Copy).then_inc(w_split, 1)
            for k in (1, 2):
                for t in range(NT):
                    act.wait_ge(power_ready, NT * (k - 1) + t + 1)
                    act.activation(ap_hi[k][:, t, :], bank_a[t][:, :], ACT.Copy).then_inc(power_hi, 1)

            def split_input(g, b):
                act.wait_ge(x_loaded[b], 16 * g + 16)
                act.wait_ge(normed[b], N_LN * g + PRIMED)
                act.activation(nodes_hi_t[:, b, :], x_in[:, b, :], ACT.Copy).then_inc(nodes_hi[b], 1)

            def agg_high(n, b):
                act.wait_ge(agg_ready[b], n)
                act.activation(agg_hi_t[:, b, :], bank_a[b][:, :], ACT.Copy).then_inc(agg_hi[b], 1)

            def reset_gate(g, s, b):
                act.wait_ge(rgate_ready, gated_count(g, s, b))
                act.wait_ge(stored[b], 16 * g + PRIMED)
                act.activation(nodes32[:, b, :], bank_b[b][:, :], ACT.Sigmoid,
                               bias=bias_r[:, :]).then_inc(r_done, 1)

            def nodes_high(g, s, b):
                act.wait_ge(nodes_ready[b], N_NODES * g + s + 1 + PRIMED)
                act.activation(nodes_hi_t[:, b, :], bank_b[b][:, :], ACT.Copy).then_inc(nodes_hi[b], 1)

            def candidate(g, s, b):
                act.wait_ge(cand_ready, gated_count(g, s, b))
                act.activation(work[:, b, N:2 * N], bank_a[b][:, :], ACT.Tanh,
                               bias=bias_h[:, :]).then_inc(cand_done, 1)

            def update_gate(g, s, b):
                act.wait_ge(zgate_ready, gated_count(g, s, b))
                act.activation(chan32[:, b, :], bank_b[b][:, :], ACT.Sigmoid,
                               bias=bias_z[:, :]).then_inc(z_done, 1)

            def gated(g, s, last=False, tail=False):
                for b in range(SLOTS):
                    if not tail:
                        agg_high(N_AGG * g + s + 1, b)
                    behind(g, s, b, tail, last)

            def behind(g, s, b, tail, last):
                first = isinstance(s, int) and s == 0
                if (b >= 1 or not first) and (not tail or b < 1):
                    s1, b1 = (s, b - 1) if b >= 1 else (s - 1, SLOTS - 1)
                    reset_gate(g, s1, b1)
                if (b >= 3 or not first) and (not tail or b < 3):
                    s3, b3 = (s, 0) if b == 3 else (s - 1, b + 1)
                    if not (tail or (last and b == 3)):
                        nodes_high(g, s3, b3)
                if (b >= 2 or not first) and (not tail or b < 2):
                    s2, b2 = (s, b - 2) if b >= 2 else (s - 1, b + 2)
                    candidate(g, s2, b2)
                if (b >= 1 or not first) and (not tail or b < 1):
                    s1, b1 = (s, b - 1) if b >= 1 else (s - 1, SLOTS - 1)
                    update_gate(g, s1, b1)

            def norm(g, k, b):
                if k < 3:
                    act.wait_ge(normed[b], N_LN * g + k + 1 + PRIMED)
                    act.activation(nodes_hi_t[:, b, :], nodes32[:, b, :], ACT.Copy).then_inc(nodes_hi[b], 1)

            def channels(g, k, b):
                act.wait_ge(chan_ready[b], N_CHAN * g + k + 1)
                act.activation(chan_hi_t[:, b, :], bank_a[b][:, :], ACT.Copy).then_inc(chan_hi[b], 1)
                act.activation(chan32[:, b, :], bank_a[b][:, :], ACT.Copy,
                               accum_out=xsum_t[:, b, :]).then_inc(chan_done[b], 1)

            def agg_high_b(n, b):
                act.wait_ge(agg_ready[b], n)
                act.activation(agg_hi_t[:, b, :], bank_b[b][:, :], ACT.Copy).then_inc(agg_hi[b], 1)

            def softmax(g, b):
                act.wait_ge(nmax_done, SLOTS * g + b + 1)
                for t in range(NT):
                    e = work[:, b, t * HALF:(t + 1) * HALF]
                    ins = act.activation(e, e, ACT.Exp, bias=nmax_t[:, b, t:t + 1], accum_out=lsum_t[:, b, t:t + 1])
                ins.then_inc(low_done, 1)
                act.wait_ge(udif_done, SLOTS * g + b + 1)
                act.activation(uexp_t[:, b, :], udif_t[:, b, :], ACT.Exp).then_inc(up_done, 1)
                act.wait_ge(hup_done, SLOTS * g + b + 1)
                act.activation(nodes_hi_t[:, b, :], row32[:, b, :], ACT.Copy).then_inc(hup_hi, 1)

            with act.Fori(0, GROUPS) as g:
                for b in range(SLOTS):
                    split_input(g, b)
                gated(g, 0)
                with act.Fori(1, STEPS - 1) as s:
                    gated(g, s)
                gated(g, STEPS - 1, last=True)
                gated(g, STEPS, tail=True)
                for phase, k, b in late_order():
                    if phase == "norm":
                        norm(g, k, b)
                    elif phase == "channels":
                        channels(g, k, b)
                    elif phase == "agg":
                        agg_high_b(N_AGG * g + STEPS + k, b)
                    elif phase == "power" and k < 3:
                        agg_high_b(N_AGG * g + STEPS + 2 + k, b)
                    elif phase == "cols":
                        act.wait_ge(cols_ready, SLOTS * g + b + 1)
                        act.activation(srow_t[:, b, :], bank_b[b][0:1, 0:P], ACT.Copy).then_inc(srow_done, 1)
                    elif phase == "rank1":
                        act.wait_ge(rank_ready, SLOTS * g + b + 1)
                        act.activation(rank_hi_t[:, b, :], bank_b[b][:, 2 * P:3 * P], ACT.Copy).then_inc(rank_hi, 1)
                    elif phase == "rows":
                        act.wait_ge(vrow_ready, SLOTS * g + b + 1)
                        act.activation(row32[:, b, :], bank_b[b][:, :], ACT.Copy, scale=LEAK).then_inc(vleak_done, 1)
                    elif phase == "softmax":
                        softmax(g, b)

        @block.vector
        def _(dve):
            dve.wait_ge(adj_split, 1)
            dve.tensor_tensor(ap_lo[0][:, :, :], adjt32[:, :, :], ap_hi[0][:, :, :].bitcast(F32),
                              ALU.subtract).then_inc(adj_split, 1)
            dve.wait_ge(adj_split, 3)
            dve.tensor_tensor(chan_lo_t[:, :, :], adj32, chan_hi_t[:, :, :].bitcast(F32),
                              ALU.subtract).then_inc(adj_split, 1)
            dve.wait_ge(w_loaded, 16)
            dve.wait_ge(cols_loaded, 16)
            dve.wait_ge(prep_small, 1)
            dve.wait_ge(consts_set, 5)
            dve.tensor_copy(wrgb[:, :], bank_b[0][:, 0:2]).then_inc(prep_small_read, 1)
            dve.tensor_copy(wo_att[:, 0:2], bank_b[1][:, 0:2]).then_inc(prep_small_read, 1)
            dve.wait_ge(prep_small_read, 2)
            dve.tensor_tensor(wo_att[:, 2:3], wo_att[:, 0:1], wo_att[:, 1:2], ALU.add).then_inc(prep_small_read, 1)
            dve.tensor_tensor(mixed[:, S_R, :], w_in[:, W4A, :], w_in[:, W4B, :], ALU.add).then_inc(prep_small_read, 1)
            dve.tensor_tensor(mixed[:, S_H, :], w_in[:, W5A, :], w_in[:, W5B, :], ALU.add)
            dve.tensor_tensor(mixed[:, S_ZR, :], w_in[:, W3A, :], w_in[:, W3B, :], ALU.add).then_inc(prep_small_read, 1)
            dve.tensor_copy(mixed[:, S_U3:S_U5 + 1, :], w_in[:, U3:U5 + 1, :])
            dve.tensor_scalar(mixed[:, S_W1, :], w_in[:, W1, :], wrgb[:, 0:1], None, ALU.mult)
            dve.tensor_copy(mixed[:, S_X0, :], w_in[:, C0, :])
            dve.tensor_tensor(mixed[:, S_X1:S_X3 + 1, :], w_in[:, C1:C3 + 1, :], w_in[:, C4:C6 + 1, :], ALU.add)
            dve.tensor_copy(mixed[:, S_WO:S_WS + 1, :], w_in[:, WO:WS + 1, :])
            dve.tensor_scalar(mixed[:, S_SJ, :], ones[:, :], cols[:, WJ:WJ + 1], None, ALU.mult)
            dve.wait_ge(prep_small_read, 3)
            dve.tensor_scalar(mixed[:, S_V, :], ones[:, :], wo_att[:, 2:3], None, ALU.mult)
            dve.tensor_scalar(mixed[:, S_P1, :], ones[:, :], wo_att[:, 0:1], None, ALU.mult)
            dve.tensor_scalar(mixed[:, S_P2, :], ones[:, :], wo_att[:, 1:2], None, ALU.mult)
            dve.tensor_tensor(bias_r[:, :], cols[:, B4:B4 + 1], cols[:, BU3:BU3 + 1], ALU.add)
            dve.tensor_tensor(bias_z[:, :], cols[:, B3:B3 + 1], cols[:, BU3:BU3 + 1], ALU.add)
            dve.tensor_tensor(bias_h[:, :], cols[:, B5:B5 + 1], cols[:, BU5:BU5 + 1], ALU.add)
            dve.wait_ge(prep_small_read, 5)
            dve.tensor_tensor(mixed[:, S_ZR, :], mixed[:, S_ZR, :], mixed[:, S_R, :], ALU.subtract).then_inc(w_mixed, 1)
            dve.wait_ge(w_split, 1)
            dve.tensor_tensor(w_lo[:, :, :], mixed, w_hi[:, :, :].bitcast(F32), ALU.subtract).then_inc(w_split, 1)
            dve.tensor_scalar(low_neg[:, :, :], adjt32[:, :, 0:HALF], 0.0, -NEG_BIG, ALU.is_gt, ALU.mult).then_inc(masks_set, 1)
            dve.tensor_scalar(up32, adjt32[:, :, HALF:N], 0.0, None, ALU.is_gt).then_inc(masks_set, 1)
            dve.wait_ge(masks_set, 2)
            dve.tensor_scalar(low_neg[:, :, :], low_neg[:, :, :], NEG_BIG, None, ALU.add).then_inc(masks_set, 1)
            dve.tensor_reduce(any_up[:, :], up32, AX_X, ALU.max).then_inc(masks_set, 1)
            dve.wait_ge(masks_set, 4)
            dve.tensor_scalar(no_up[:, :], any_up[:, :], -1.0, 1.0, ALU.mult, ALU.add).then_inc(masks_set, 1)
            dve.wait_ge(masks_set, 5)
            dve.tensor_scalar(up_neg[:, :], no_up[:, :], NEG_BIG, None, ALU.mult)
            for t in range(NT):
                dve.tensor_scalar(up_mask[:, t, :], up32[:, t, :], no_up[:, t:t + 1], None, ALU.max).then_inc(masks_set, 1)
            dve.wait_ge(masks_set, 5 + NT)
            dve.tensor_reduce(up_count[:, :], up_mask[:, :, :].bitcast(F32), AX_X, ALU.add).then_inc(masks_set, 1)
            dve.wait_ge(masks_set, 6 + NT)
            for k in (1, 2):
                for t in range(NT):
                    dve.wait_ge(power_hi, NT * (k - 1) + t + 1)
                    dve.tensor_tensor(ap_lo[k][:, t, :], bank_a[t][:, :], ap_hi[k][:, t, :].bitcast(F32),
                                      ALU.subtract).then_inc(power_lo, 1)

            def split_input(g, b):
                dve.wait_ge(nodes_hi[b], N_SPLIT * g + 1)
                dve.tensor_tensor(nodes_lo_t[:, b, :], x_in[:, b, :], nodes_hi_t[:, b, :].bitcast(F32),
                                  ALU.subtract).then_inc(nodes_lo[b], 1)

            def agg_low(n, b, bank):
                dve.wait_ge(agg_hi[b], n)
                dve.tensor_tensor(agg_lo_t[:, b, :], bank[b][:, :], agg_hi_t[:, b, :].bitcast(F32),
                                  ALU.subtract).then_inc(agg_lo[b], 1)

            def reset_state(g, s, b):
                dve.wait_ge(h_loaded[b], 16 * g + 16)
                dve.wait_ge(r_done, gated_count(g, s, b))
                dve.tensor_tensor(work[:, b, 0:N], nodes32[:, b, :], h_ch[:, b, :], ALU.mult).then_inc(rh_done, 1)

            def nodes_low(g, s, b):
                dve.wait_ge(nodes_hi[b], N_SPLIT * g + s + 2)
                dve.tensor_tensor(nodes_lo_t[:, b, :], bank_b[b][:, :], nodes_hi_t[:, b, :].bitcast(F32),
                                  ALU.subtract).then_inc(nodes_lo[b], 1)

            def new_state(g, s, b):
                n = gated_count(g, s, b)
                cand = work[:, b, N:2 * N]
                dve.wait_ge(cand_done, n)
                dve.tensor_tensor(cand, cand, h_ch[:, b, :], ALU.subtract).then_inc(delta_done, 1)
                dve.wait_ge(z_done, n)
                dve.wait_ge(delta_done, n)
                dve.tensor_tensor(cand, cand, chan32[:, b, :], ALU.mult).then_inc(gated_done, 1)
                dve.wait_ge(gated_done, n)
                dve.tensor_tensor(h_ch[:, b, :], h_ch[:, b, :], cand, ALU.add).then_inc(h_done[b], 1)

            def gated(g, s, last=False, tail=False):
                first = isinstance(s, int) and s == 0
                for b in range(SLOTS):
                    if not tail:
                        agg_low(N_AGG * g + s + 1, b, bank_a)
                    if (b >= 1 or not first) and (not tail or b < 1):
                        s1, b1 = (s, b - 1) if b >= 1 else (s - 1, SLOTS - 1)
                        reset_state(g, s1, b1)
                    if (b >= 3 or not first) and not (tail or (last and b == 3)):
                        s3, b3 = (s, 0) if b == 3 else (s - 1, b + 1)
                        nodes_low(g, s3, b3)
                    if (b >= 2 or not first) and (not tail or b < 2):
                        s2, b2 = (s, b - 2) if b >= 2 else (s - 1, b + 2)
                        new_state(g, s2, b2)

            def norm(g, k, b):
                n = N_LN * g + k + 1
                if k == 0:
                    dve.wait_ge(nodes_ready[b], N_NODES * g + STEPS + PRIMED)
                    dve.tensor_tensor(nodes32[:, b, :], bank_b[b][:, :], x_in[:, b, :], ALU.add).then_inc(first_sum, 1)
                    dve.wait_ge(first_sum, SLOTS * g + b + 1 + PRIMED)
                    y = nodes32[:, b, :]
                else:
                    dve.wait_ge(nodes_ready[b], N_NODES * g + STEPS + k + PRIMED)
                    y = bank_b[b][:, :]
                for t in range(NT):
                    dve.bn_stats(stats_t[:, b, t, :], y[:, t * P:(t + 1) * P])
                dve.drain()
                for t in range(NT):
                    ins = dve.bn_aggr(moments_t[:, b, t, :], stats_t[:, b, t, :])
                ins.then_inc(moments_done, 1)
                dve.wait_ge(rstd_done, norm_count(g, k, b))
                dve.wait_ge(moments_done, norm_count(g, k, b))
                for t in range(NT):
                    ins = dve.tensor_scalar(nodes32[:, b, t * P:(t + 1) * P], y[:, t * P:(t + 1) * P],
                                            moments_t[:, b, t, 0:1], rstd_t[:, b, t:t + 1],
                                            ALU.subtract, ALU.mult)
                ins.then_inc(normed[b], 1)
                if k < 3:
                    dve.wait_ge(nodes_hi[b], N_SPLIT * g + STEPS + k + 1)
                    dve.wait_ge(normed[b], N_LN * g + k + 1 + PRIMED)
                    dve.tensor_tensor(nodes_lo_t[:, b, :], nodes32[:, b, :], nodes_hi_t[:, b, :].bitcast(F32),
                                      ALU.subtract).then_inc(nodes_lo[b], 1)

            def channels(g, k, b):
                dve.wait_ge(chan_hi[b], N_CHAN * g + k + 1)
                dve.wait_ge(chan_done[b], N_CHAN * g + k + 1)
                dve.tensor_tensor(chan_lo_t[:, b, :], chan32[:, b, :], chan_hi_t[:, b, :].bitcast(F32),
                                  ALU.subtract).then_inc(chan_lo[b], 1)

            def relation_sums(g, b):
                n = SLOTS * g + b + 1
                dve.wait_ge(sj_ready, n)
                dve.wait_ge(chan_done[b], N_CHAN * g + 1)
                dve.tensor_tensor_reduce(trash[:, :], bank_a[b][:, :], chan32[:, b, :], 1.0, 0.0,
                                         ALU.mult, ALU.add, tcol_t[:, b, :]).then_inc(t_done, 1)
                dve.wait_ge(t_done, n)
                dve.scalar_tensor_tensor(out=mix_t[:, b, :], in0=xsum_t[:, b, :], scalar=wrgb[:, 1:2],
                                         in1=tcol_t[:, b, :], op0=ALU.mult, op1=ALU.add).then_inc(mix_done, 1)

            def residual(g, k, b, bank, scalar):
                dve.wait_ge(out_ready[b], N_OUT * g + k)
                dve.scalar_tensor_tensor(out=row32[:, b, :], in0=bank[b][:, :], scalar=scalar,
                                         in1=chan32[:, b, :], op0=ALU.add, op1=ALU.add).then_inc(resid_done[b], 1)

            def logits(g, b):
                n = SLOTS * g + b + 1
                dve.wait_ge(vleak_done, n)
                dve.tensor_tensor(row32[:, b, :], bank_b[b][:, :], row32[:, b, :], ALU.max).then_inc(vrow_done, 1)
                dve.wait_ge(pair_ready, n)
                for c in range(2):
                    if c:
                        dve.wait_ge(pair_done, 2 * n - 1)
                    dve.tensor_tensor_reduce(trash[:, 0:P], bank_a[b][:, c * P:(c + 1) * P], ident[:, :], 1.0, 0.0,
                                             ALU.mult, ALU.add, pair_t[:, b, c:c + 1]).then_inc(pair_done, 1)
                dve.wait_ge(pair_done, 2 * n)
                dve.scalar_tensor_tensor(out=pairl_t[:, b, :], in0=pair_t[:, b, :], scalar=LEAK,
                                         in1=pair_t[:, b, :], op0=ALU.mult, op1=ALU.max).then_inc(pairl_done, 1)

            def softmax(g, b):
                n = SLOTS * g + b + 1
                dve.wait_ge(vrow_done, n)
                dve.wait_ge(pairl_done, n)
                for c in range(2):
                    ins = dve.tensor_tensor(umax_t[:, b, 2 * c:2 * c + 2], pairl_t[:, b, :],
                                            up_neg[:, 2 * c:2 * c + 2], ALU.add)
                ins.then_inc(umax_done, 1)
                for t in range(NT):
                    ins = dve.tensor_tensor_reduce(work[:, b, t * HALF:(t + 1) * HALF],
                                                   row32[:, b, t // 2:N:2], low_neg[:, t, :], 1.0, 3 * NEG_BIG,
                                                   ALU.add, ALU.max, lmax_t[:, b, t:t + 1])
                ins.then_inc(lmax_done, 1)
                dve.wait_ge(lmax_done, n)
                dve.wait_ge(umax_done, n)
                dve.tensor_tensor(lmax_t[:, b, :], lmax_t[:, b, :], umax_t[:, b, :], ALU.max).then_inc(lmax2_done, 1)
                dve.wait_ge(lmax2_done, n)
                dve.tensor_scalar(nmax_t[:, b, :], lmax_t[:, b, :], -1.0, None, ALU.mult).then_inc(nmax_done, 1)
                dve.tensor_tensor(udif_t[:, b, :], umax_t[:, b, :], lmax_t[:, b, :], ALU.subtract).then_inc(udif_done, 1)
                dve.wait_ge(up_done, n)
                dve.tensor_tensor(usum_t[:, b, :], uexp_t[:, b, :], up_count[:, :], ALU.mult).then_inc(usum_done, 1)
                dve.wait_ge(usum_done, n)
                dve.wait_ge(low_done, n)
                dve.tensor_tensor(den_t[:, b, :], usum_t[:, b, :], lsum_t[:, b, :], ALU.add).then_inc(den_done, 1)
                dve.wait_ge(den_done, n)
                dve.reciprocal(rden_t[:, b, :], den_t[:, b, :]).then_inc(rden_done, 1)
                dve.wait_ge(rden_done, n)
                dve.tensor_tensor(uden_t[:, b, :], uexp_t[:, b, :], rden_t[:, b, :], ALU.mult).then_inc(uden_done, 1)
                dve.wait_ge(att_ready, n)
                dve.wait_ge(uden_done, n)
                h = bank_a[b][:, :].rearrange("p (t c) -> p t c", t=NT)
                dve.tensor_tensor(row32[:, b, :].rearrange("p (t c) -> p t c", t=NT), h,
                                  uden_t[:, b, :].unsqueeze(2).to_broadcast([P, NT, P]), ALU.mult).then_inc(hup_done, 1)
                dve.tensor_tensor(nodes32[:, b, :].rearrange("p (t c) -> p t c", t=NT), h,
                                  rden_t[:, b, :].unsqueeze(2).to_broadcast([P, NT, P]), ALU.mult).then_inc(hlow_done, 1)
                dve.wait_ge(hup_hi, n)
                dve.tensor_tensor(nodes_lo_t[:, b, :], row32[:, b, :], nodes_hi_t[:, b, :].bitcast(F32),
                                  ALU.subtract).then_inc(hup_lo, 1)

            with dve.Fori(0, GROUPS) as g:
                for b in range(SLOTS):
                    split_input(g, b)
                gated(g, 0)
                with dve.Fori(1, STEPS - 1) as s:
                    gated(g, s)
                gated(g, STEPS - 1, last=True)
                gated(g, STEPS, tail=True)
                for phase, k, b in late_order():
                    if phase == "norm":
                        norm(g, k, b)
                    elif phase == "channels":
                        channels(g, k, b)
                    elif phase == "agg":
                        agg_low(N_AGG * g + STEPS + k, b, bank_b)
                    elif phase == "power":
                        if k < 3:
                            agg_low(N_AGG * g + STEPS + 2 + k, b, bank_b)
                        else:
                            residual(g, 2, b, bank_a, 0.0)
                    elif phase == "sj":
                        relation_sums(g, b)
                    elif phase == "cols":
                        dve.wait_ge(srow_done, SLOTS * g + b + 1)
                        dve.tensor_tensor(ccol_t[:, b, :], bank_b[b][:, P:P + 1], cols[:, BIAS1:BIAS1 + 1],
                                          ALU.add).then_inc(ccol_done, 1)
                    elif phase == "rank1":
                        dve.wait_ge(rank_hi, SLOTS * g + b + 1)
                        dve.tensor_tensor(rank_lo_t[:, b, :], bank_b[b][:, 2 * P:3 * P],
                                          rank_hi_t[:, b, :].bitcast(F32), ALU.subtract).then_inc(rank_lo, 1)
                    elif phase == "out1":
                        dve.wait_ge(ccol_done, SLOTS * g + b + 1)
                        residual(g, 1, b, bank_a, ccol_t[:, b, :])
                    elif phase == "rows":
                        logits(g, b)
                    elif phase == "softmax":
                        softmax(g, b)
                    elif phase == "attend":
                        residual(g, 3, b, bank_b, 0.0)

        @block.tensor
        def _(pe):
            def split_product(psum, lhs, rhs, start, stop):
                pe.matmul(psum, lhs[0], rhs[0], start=start, stop=False)
                pe.matmul(psum, lhs[0], rhs[1], start=False, stop=False)
                return pe.matmul(psum, lhs[1], rhs[0], start=False, stop=stop)

            def weight(n):
                return w_hi[:, n, :], w_lo[:, n, :]

            def tile_of(hi, lo, b, t):
                return hi[:, b, t * P:(t + 1) * P], lo[:, b, t * P:(t + 1) * P]

            def neighbours(b, k, psum):
                for t in range(NT):
                    ins = split_product(psum, tile_of(nodes_hi_t, nodes_lo_t, b, t),
                                        (ap_hi[k - 1][:, t, :], ap_lo[k - 1][:, t, :]), t == 0, t == NT - 1)
                ins.then_inc(agg_ready[b], 1)

            def turn(psum, source):
                for t in range(NT):
                    ins = pe.transpose(psum[:, t * P:(t + 1) * P], source[:, t * P:(t + 1) * P], ident[:, :])
                return ins

            pe.wait_ge(consts_set, 5)
            pe.wait_ge(rows_loaded, 16)
            pe.matmul(bank_b[0][:, 0:2], ones[0:1, :], rows[:, P:P + 2], start=True, stop=True)
            pe.wait_ge(w_loaded, 16)
            pe.wait_ge(cols_loaded, 16)
            pe.matmul(bank_b[1][:, 0:2], w_in[:, WOT, :], cols[:, A1:A2 + 1], start=True, stop=True).then_inc(prep_small, 1)
            pe.wait_ge(adj_split, 4)
            for k in (1, 2):
                if k == 2:
                    pe.wait_ge(power_lo, NT)
                for m in range(NT):
                    for t in range(NT):
                        ins = split_product(bank_a[m][:, :], tile_of(chan_hi_t, chan_lo_t, t, m),
                                            (ap_hi[k - 1][:, t, :], ap_lo[k - 1][:, t, :]), t == 0, t == NT - 1)
                    ins.then_inc(power_ready, 1)
            pe.wait_ge(w_split, 2)
            pe.wait_ge(power_lo, 2 * NT)

            def gate_r(g, s, b):
                pe.wait_ge(agg_lo[b], N_AGG * g + s + 1)
                pe.wait_ge(h_loaded[b], 16 * g + 16)
                pe.wait_ge(normed[b], N_LN * g + PRIMED)
                h = h_ch[:, b, :]
                agg = (agg_hi_t[:, b, :], agg_lo_t[:, b, :])
                split_product(bank_b[b][:, :], weight(S_R), agg, True, False)
                pe.matmul(bank_b[b][:, :], w_in[:, U3, :], h, start=False, stop=True).then_inc(rgate_ready, 1)

            def gate_z(g, s, b):
                pe.wait_ge(r_done, gated_count(g, s, b))
                for w, a, last in ((w_hi, agg_hi_t, False), (w_hi, agg_lo_t, False), (w_lo, agg_hi_t, True)):
                    ins = pe.matmul(bank_b[b][:, :], w[:, S_ZR, :], a[:, b, :], start=False, stop=last,
                                    skip_group_check=True)
                ins.then_inc(zgate_ready, 1)

            def candidate_agg(b):
                split_product(bank_a[b][:, :], weight(S_H), (agg_hi_t[:, b, :], agg_lo_t[:, b, :]), True, False)

            def candidate_state(g, s, b):
                pe.wait_ge(rh_done, gated_count(g, s, b))
                pe.matmul(bank_a[b][:, :], w_in[:, U5, :], work[:, b, 0:N],
                          start=False, stop=True).then_inc(cand_ready, 1)

            def gated(g, s, tail=False):
                first = isinstance(s, int) and s == 0
                for b in range(SLOTS):
                    if not tail:
                        pe.wait_ge(nodes_lo[b], N_SPLIT * g + s + 1)
                        neighbours(b, 1, bank_a[b][:, :])
                    one = (b >= 1 or not first) and (not tail or b < 1)
                    s1, b1 = (s, b - 1) if b >= 1 else (s - 1, SLOTS - 1)
                    if one:
                        gate_r(g, s1, b1)
                    if (b >= 3 or not first) and (not tail or b < 3):
                        s3, b3 = (s, 0) if b == 3 else (s - 1, b + 1)
                        pe.wait_ge(h_done[b3], STEPS * g + s3 + 1)
                        turn(bank_b[b3], h_ch[:, b3, :]).then_inc(nodes_ready[b3], 1)
                    if one:
                        candidate_agg(b1)
                    if (b >= 2 or not first) and (not tail or b < 2):
                        s2, b2 = (s, b - 2) if b >= 2 else (s - 1, b + 2)
                        candidate_state(g, s2, b2)
                    if one:
                        gate_z(g, s1, b1)

            def power(g, k, b):
                pe.wait_ge(agg_lo[b], N_AGG * g + STEPS + 1 + k)
                if k == 1:
                    pe.wait_ge(chan_lo[b], N_CHAN * g + 2)
                    pe.wait_ge(chan_done[b], N_CHAN * g + 2)
                    split_product(bank_a[b][:, :], weight(S_X0), (chan_hi_t[:, b, :], chan_lo_t[:, b, :]), True, False)
                ins = split_product(bank_a[b][:, :], weight(S_X0 + k), (agg_hi_t[:, b, :], agg_lo_t[:, b, :]), False, k == 3)
                if k == 3:
                    ins.then_inc(out_ready[b], 1)
                else:
                    neighbours(b, k + 1, bank_b[b][:, :])

            def att_rows(g, b):
                x = (chan_hi_t[:, b, :], chan_lo_t[:, b, :])
                even = tuple(v[:, 0:N:2] for v in x)
                odd = tuple(v[:, 1:N:2] for v in x)
                pe.wait_ge(chan_lo[b], N_CHAN * g + 3)
                pe.wait_ge(chan_done[b], N_CHAN * g + 3)
                split_product(bank_b[b][:, :], weight(S_V), x, True, True).then_inc(vrow_ready, 1)
                split_product(bank_a[b][:, 0:HALF], weight(S_P1), even, True, False)
                split_product(bank_a[b][:, 0:HALF], weight(S_P2), odd, False, True).then_inc(pair_ready, 1)

            def att_values(g, b):
                pe.wait_ge(pair_done, 2 * (SLOTS * g + b + 1))
                for t in range(NT):
                    ins = split_product(bank_a[b][:, t * P:(t + 1) * P], tile_of(chan_hi_t, chan_lo_t, b, t),
                                        weight(S_WO), True, True)
                ins.then_inc(att_ready, 1)
                pe.wait_ge(vrow_done, SLOTS * g + b + 1)
                split_product(bank_b[b][:, :], weight(S_WS), (chan_hi_t[:, b, :], chan_lo_t[:, b, :]), True, False)

            def attend(g, b):
                n = SLOTS * g + b + 1
                pe.wait_ge(hlow_done, n)
                for t in range(NT):
                    pe.matmul(bank_b[b][:, 0:HALF], nodes32[:, b, t * P:(t + 1) * P],
                              work[:, b, t * HALF:(t + 1) * HALF], start=False, stop=False)
                pe.wait_ge(hup_lo, n)
                for t in range(NT):
                    hi, lo = tile_of(nodes_hi_t, nodes_lo_t, b, t)
                    pe.matmul(bank_b[b][:, HALF:N], hi, up_mask[:, t, :], start=False, stop=False)
                    ins = pe.matmul(bank_b[b][:, HALF:N], lo, up_mask[:, t, :], start=False, stop=(t == NT - 1))
                ins.then_inc(out_ready[b], 1)

            with pe.Fori(0, GROUPS) as g:
                gated(g, 0)
                with pe.Fori(1, STEPS - 1) as s:
                    gated(g, s)
                gated(g, STEPS - 1)
                gated(g, STEPS, tail=True)
                for phase, k, b in late_order():
                    n = SLOTS * g + b + 1
                    if phase == "channels":
                        pe.wait_ge(normed[b], N_LN * g + k + 1 + PRIMED)
                        turn(bank_a[b], nodes32[:, b, :]).then_inc(chan_ready[b], 1)
                    elif phase == "turn":
                        pe.wait_ge(resid_done[b], N_OUT * g + k)
                        turn(bank_b[b], row32[:, b, :]).then_inc(nodes_ready[b], 1)
                    elif phase == "agg":
                        pe.wait_ge(nodes_lo[b], N_SPLIT * g + STEPS + k)
                        neighbours(b, 1, bank_b[b][:, :])
                    elif phase == "sj":
                        pe.wait_ge(chan_lo[b], N_CHAN * g + 1)
                        pe.wait_ge(chan_done[b], N_CHAN * g + 1)
                        split_product(bank_a[b][:, :], weight(S_SJ), (chan_hi_t[:, b, :], chan_lo_t[:, b, :]),
                                      True, True).then_inc(sj_ready, 1)
                    elif phase == "cols":
                        pe.wait_ge(agg_lo[b], N_AGG * g + STEPS + 1)
                        pe.wait_ge(mix_done, n)
                        pe.matmul(bank_b[b][0:1, 0:P], xsum_t[:, b, :], w_in[:, W1, :], start=True, stop=True)
                        pe.matmul(bank_b[b][:, P:P + 1], w_in[:, W1, :], mix_t[:, b, :], start=True,
                                  stop=True).then_inc(cols_ready, 1)
                    elif phase == "rank1":
                        pe.wait_ge(srow_done, n)
                        pe.wait_ge(ccol_done, n)
                        pe.matmul(bank_b[b][:, 2 * P:3 * P], rows[:, 0:P], srow_t[:, b, :], start=True,
                                  stop=True).then_inc(rank_ready, 1)
                    elif phase == "out1":
                        pe.wait_ge(rank_lo, n)
                        split_product(bank_a[b][:, :], weight(S_W1), (agg_hi_t[:, b, :], agg_lo_t[:, b, :]), True, False)
                        split_product(bank_a[b][:, :], (rank_hi_t[:, b, :], rank_lo_t[:, b, :]),
                                      (chan_hi_t[:, b, :], chan_lo_t[:, b, :]), False, True).then_inc(out_ready[b], 1)
                    elif phase == "power":
                        power(g, k, b)
                    elif phase == "rows":
                        att_rows(g, b)
                    elif phase == "softmax":
                        att_values(g, b)
                    elif phase == "attend":
                        attend(g, b)


def kernel(x, adj, L0_gnn_w3_w, L0_gnn_w3_b, L0_gnn_u3_w, L0_gnn_u3_b, L0_gnn_w4_w, L0_gnn_w4_b, L0_gnn_w5_w,
           L0_gnn_w5_b, L0_gnn_u5_w, L0_gnn_u5_b, L1_gnn_g_w, L1_gnn_g_b, L1_gnn_weight, L1_gnn_bias,
           L2_gnn_weight_1, L3_gnn_others_weight, L3_gnn_self_weight, L3_gnn_att_weight):
    import numpy as np
    import concourse.bacc as bacc
    from concourse.bass_utils import run_bass_kernel_spmd

    def halves(w):
        w = np.asarray(w)
        return [w[:, :P].T, w[:, P:].T]

    stacked = [*halves(L0_gnn_w3_w), *halves(L0_gnn_w4_w), *halves(L0_gnn_w5_w),
               np.asarray(L0_gnn_u3_w).T, np.asarray(L0_gnn_u5_w).T, np.asarray(L1_gnn_weight),
               *[np.asarray(L2_gnn_weight_1)[:, :, k] for k in range(7)],
               np.asarray(L3_gnn_others_weight), np.asarray(L3_gnn_self_weight), np.asarray(L3_gnn_others_weight).T]
    g_w = np.asarray(L1_gnn_g_w)
    att = np.asarray(L3_gnn_att_weight)[:, 0]
    columns = [np.asarray(v) for v in (L0_gnn_w3_b, L0_gnn_w4_b, L0_gnn_w5_b, L0_gnn_u3_b, L0_gnn_u5_b)]
    columns += [g_w[:P], np.asarray(L1_gnn_bias), att[:P], att[P:]]
    row = np.concatenate([g_w[P:], np.asarray(L1_gnn_g_b).reshape(1)])[None, :]
    arrays = {
        "x_nodes": np.ascontiguousarray(x),
        "x_channels": np.ascontiguousarray(np.asarray(x).transpose(0, 2, 1)),
        "adj": np.ascontiguousarray(adj),
        "adj_t": np.ascontiguousarray(np.asarray(adj).T),
        "weights": np.ascontiguousarray(np.stack(stacked, axis=1)),
        "columns": np.ascontiguousarray(np.stack(columns, axis=1)),
        "row_in": np.ascontiguousarray(row),
    }
    nc = bacc.Bacc("TRN2", target_bir_lowering=False, num_devices=1)
    args = [nc.dram_tensor(name, a.shape, mybir.dt.from_np(a.dtype), kind="ExternalInput").ap()
            for name, a in arrays.items()]
    out = nc.dram_tensor("out", (BATCH, N, P), F32, kind="ExternalOutput").ap()
    build(nc, *args, out)
    result = run_bass_kernel_spmd(nc, [arrays], core_ids=[0])
    return result.results[0]["out"]
```

```python
from contextlib import ExitStack

import concourse.bass as bass
from concourse import mybir

F32 = mybir.dt.float32
F32R = mybir.dt.float32r
ALU = mybir.AluOpType
ACT = mybir.ActivationFunctionType
AX_X = mybir.AxisListType.X

P = 128
N = 512
NT = N // P
HALF = N // 2
BATCH = 32
SLOTS = 4
GROUPS = BATCH // SLOTS
STEPS = 5
EPS = 1e-5
NEG_BIG = -9000000000000000.0
LEAK = 0.1

(W3A, W3B, W4A, W4B, W5A, W5B, U3, U5, W1, C0, C1, C2, C3, C4, C5, C6, WO, WS, WOT) = range(19)
(B3, B4, B5, BU3, BU5, WJ, BIAS1, A1, A2) = range(9)
(S_R, S_H, S_ZR, S_U3, S_U5, S_W1, S_X0, S_X1, S_X2, S_X3, S_WO, S_WS, S_SJ, S_V, S_P1, S_P2) = range(16)

N_AGG = STEPS + 1 + 3
N_NODES = STEPS + 3
N_SPLIT = STEPS + 3
N_LN = 4
N_CHAN = 3
N_OUT = 3


PAIRS = ((0, 1), (2, 3))
TURNS = 2 * STEPS

PRIMED = 1


def gated_count(g, i, b):
    return SLOTS * STEPS * g + TURNS * (b // 2) + i + 1


LATE = (
    (("norm", 0),),
    (("channels", 0),), (("agg", 1), ("sj", 1)), (("cols", 1),), (("rank1", 1),), (("out1", 1),),
    (("turn", 1), ("norm", 1)),
    (("channels", 1),), (("agg", 2),), (("power", 1),), (("power", 2),), (("power", 3),),
    (("turn", 2), ("norm", 2)),
    (("channels", 2),), (("rows", 3),), (("weights", 3),), (("values", 3),), (("attend", 3),),
    (("turn", 3), ("norm", 3), ("refill", 0)),
)
LAST_SPOT = 2 * TURNS - 1
POWER_SPOTS = (1, 2, 3, 4, 8, 9, 10, 11)
MASK_SPOT = 6
NORM_TURNS = [(k, b) for spot in range(len(LATE) + 1) for b in (0, 1) if 0 <= spot - b < len(LATE)
              for phase, k in LATE[spot - b] if phase == "norm"]


def norm_count(g, k, b):
    return N_LN * SLOTS * g + len(NORM_TURNS) * (b // 2) + NORM_TURNS.index((k, b % 2)) + 1


def late_spot(spot, late):
    if late:
        g, pair = late
        for b in (0, 1):
            if 0 <= spot - b < len(LATE):
                for phase, k in LATE[spot - b]:
                    yield phase, g, k, pair[b]


def turns(gated, late):
    for i in range(TURNS):
        now = (gated[0], i, gated[1][i % 2]) if gated else None
        before = (gated[0], i - 1, gated[1][(i - 1) % 2]) if gated and i else None
        if i == 0 and late:
            before = (late[0], TURNS - 1, late[1][1])
        yield i, now, before


def build(nc, x_nodes, x_channels, adj, adj_t, weights, columns, row_in, out):
    with ExitStack() as ctx:
        def sb(name, shape, dt=F32):
            return ctx.enter_context(nc.sbuf_tensor(name, shape, dt))

        def sem(name):
            return ctx.enter_context(nc.semaphore(name))

        def sems(name):
            return [sem(f"{name}{b}") for b in range(SLOTS)]

        ap_hi = [sb(f"adj{k}_hi", [P, NT, N], F32R) for k in (1, 2, 3)]
        ap_lo = [sb(f"adj{k}_lo", [P, NT, N], F32R) for k in (1, 2, 3)]
        w_in = sb("w_in", [P, 19, P])
        w_hi = sb("w_hi", [P, 16, P], F32R)
        w_lo = sb("w_lo", [P, 16, P], F32R)
        cols = sb("cols", [P, 9])
        rows = sb("rows", [1, P + 2])
        wrgb = sb("wrgb", [P, 2])
        ident = sb("ident", [P, P])
        ones = sb("ones", [P, P])
        bias_r = sb("bias_r", [P, 1])
        bias_z = sb("bias_z", [P, 1])
        bias_h = sb("bias_h", [P, 1])
        bias_in = sb("bias_in", [P, 2])
        u5_half = sb("u5_half", [P, P])
        wo_att = sb("wo_att", [P, 3])
        half_neg = sb("half_neg", [P, NT])
        eps = sb("eps", [P, NT])
        low_neg = sb("low_neg", [P, NT, HALF])
        up_mask = sb("up_mask", [P, NT, HALF], F32R)
        no_up = sb("no_up", [P, NT])
        any_up = sb("any_up", [P, NT])
        up_neg = sb("up_neg", [P, NT])
        up_count = sb("up_count", [P, NT])

        x_in = sb("x_in", [P, SLOTS, N])
        h_ch = sb("h_ch", [P, SLOTS, N])
        chan32 = sb("chan32", [P, SLOTS, N])
        nodes32 = sb("nodes32", [P, SLOTS, N])
        work = sb("work", [P, SLOTS, 2 * N])
        row32 = sb("row32", [P, SLOTS, N])
        nodes_hi_t = sb("nodes_hi_t", [P, SLOTS, N], F32R)
        nodes_lo_t = sb("nodes_lo_t", [P, SLOTS, N], F32R)
        agg_hi_t = sb("agg_hi_t", [P, SLOTS, N], F32R)
        agg_lo_t = sb("agg_lo_t", [P, SLOTS, N], F32R)
        chan_hi_t = sb("chan_hi_t", [P, SLOTS, N], F32R)
        chan_lo_t = sb("chan_lo_t", [P, SLOTS, N], F32R)
        rank_hi_t = sb("rank_hi_t", [P, SLOTS, P], F32R)
        rank_lo_t = sb("rank_lo_t", [P, SLOTS, P], F32R)
        stats_t = sb("stats_t", [P, SLOTS, NT, 6])
        moments_t = sb("moments_t", [P, SLOTS, NT, 2])
        var_t = sb("var_t", [P, SLOTS, NT])
        rstd_t = sb("rstd_t", [P, SLOTS, NT])
        xsum_t = sb("xsum_t", [P, SLOTS, 1])
        tcol_t = sb("tcol_t", [P, SLOTS, 1])
        mix_t = sb("mix_t", [P, SLOTS, 1])
        ccol_t = sb("ccol_t", [P, SLOTS, 1])
        srow_t = sb("srow_t", [1, SLOTS, P])
        trash = sb("trash", [P, N])
        pair_t = sb("pair_t", [P, SLOTS, 2])
        pairl_t = sb("pairl_t", [P, SLOTS, 2])
        lmax_t = sb("lmax_t", [P, SLOTS, NT])
        umax_t = sb("umax_t", [P, SLOTS, NT])
        nmax_t = sb("nmax_t", [P, SLOTS, NT])
        udif_t = sb("udif_t", [P, SLOTS, NT])
        lsum_t = sb("lsum_t", [P, SLOTS, NT])
        uexp_t = sb("uexp_t", [P, SLOTS, NT])
        usum_t = sb("usum_t", [P, SLOTS, NT])
        den_t = sb("den_t", [P, SLOTS, NT])
        rden_t = sb("rden_t", [P, SLOTS, NT])
        uden_t = sb("uden_t", [P, SLOTS, NT])

        bank_a = [ctx.enter_context(nc.psum_tensor(f"bank_a{b}", [P, N], F32)) for b in range(SLOTS)]
        bank_b = [ctx.enter_context(nc.psum_tensor(f"bank_b{b}", [P, N], F32)) for b in range(SLOTS)]

        adj_loaded, adjt_loaded, w_loaded, cols_loaded, rows_loaded = (
            sem(n) for n in ("adj_loaded", "adjt_loaded", "w_loaded", "cols_loaded", "rows_loaded"))
        adjt_hi, adjt_lo, adjn_hi, adjn_lo = (sem(n) for n in ("adjt_hi", "adjt_lo", "adjn_hi", "adjn_lo"))
        consts_set, bias_sum, w_mixed, w_split, masks_set = (
            sem(n) for n in ("consts_set", "bias_sum", "w_mixed", "w_split", "masks_set"))
        prep_small, prep_small_read, power_ready, power_hi, power_lo = (
            sem(n) for n in ("prep_small", "prep_small_read", "power_ready", "power_hi", "power_lo"))
        x_loaded, h_loaded, stored = sems("x_loaded"), sems("h_loaded"), sems("stored")
        agg_ready, agg_hi, agg_lo = sems("agg_ready"), sems("agg_hi"), sems("agg_lo")
        h_done = sems("h_done")
        nodes_ready, nodes_hi, nodes_lo = sems("nodes_ready"), sems("nodes_hi"), sems("nodes_lo")
        normed = sems("normed")
        chan_ready, chan_done, chan_hi, chan_lo = (
            sems(n) for n in ("chan_ready", "chan_done", "chan_hi", "chan_lo"))
        out_ready, resid_done = sems("out_ready"), sems("resid_done")
        rgate_ready, r_done, rh_done = sem("rgate_ready"), sem("r_done"), sem("rh_done")
        zgate_ready, z_done = sem("zgate_ready"), sem("z_done")
        cand_ready, cand_done = sem("cand_ready"), sem("cand_done")
        delta_done, gated_done = sem("delta_done"), sem("gated_done")
        moments_done, var_done, rstd_done = (
            sem(n) for n in ("moments_done", "var_done", "rstd_done"))
        first_sum = sem("first_sum")
        sj_ready, t_done, mix_done = sem("sj_ready"), sem("t_done"), sem("mix_done")
        cols_ready, srow_done, ccol_done = sem("cols_ready"), sem("srow_done"), sem("ccol_done")
        rank_ready, rank_hi, rank_lo = sem("rank_ready"), sem("rank_hi"), sem("rank_lo")
        vrow_ready, vleak_done, vrow_done = sem("vrow_ready"), sem("vleak_done"), sem("vrow_done")
        pair_ready, pair_done, pairl_done = sem("pair_ready"), sem("pair_done"), sem("pairl_done")
        lmax_done, umax_done, lmax2_done, nmax_done, udif_done = (
            sem(n) for n in ("lmax_done", "umax_done", "lmax2_done", "nmax_done", "udif_done"))
        low_done, up_done, usum_done, den_done, rden_done, uden_done = (
            sem(n) for n in ("low_done", "up_done", "usum_done", "den_done", "rden_done", "uden_done"))
        att_ready, hlow_done, hup_done, hup_hi, hup_lo = (
            sem(n) for n in ("att_ready", "hlow_done", "hup_done", "hup_hi", "hup_lo"))

        adj32 = work[:, 0:2, :].rearrange("p s (t n) -> p (s t) n", t=2)
        mixed = work[:, 2:4, :].rearrange("p s (w o) -> p (s w) o", o=P)
        adjt32 = row32
        up32 = work[:, 3, :].rearrange("p (t n) -> p t n", t=NT)
        power_bank = [bank_a[2], bank_b[2], bank_a[3], bank_b[3]]

        block = ctx.enter_context(nc.Block())

        @block.sync
        def _(sp):
            for b in range(SLOTS):
                sp.sem_inc(normed[b], PRIMED)
                sp.sem_inc(stored[b], PRIMED)

            def load(g, b):
                sp.dma_start(x_in[:, b, :].rearrange("p (t c) -> p t c", t=NT),
                             x_nodes[g * SLOTS + b].rearrange("(t p) c -> p t c", p=P)).then_inc(x_loaded[b], 16)
                sp.dma_start(h_ch[:, b, :], x_channels[g * SLOTS + b]).then_inc(h_loaded[b], 16)

            def reload(g, b):
                sp.wait_ge(first_sum, SLOTS * g + b + 1)
                sp.wait_ge(nodes_ready[b], N_NODES * g + STEPS)
                load(g + 1, b)

            def store(g, b):
                sp.wait_ge(normed[b], N_LN * g + N_LN + PRIMED)
                sp.dma_start(out[g * SLOTS + b].rearrange("(t p) c -> p t c", p=P),
                             nodes32[:, b, :].rearrange("p (t c) -> p t c", t=NT)).then_inc(stored[b], 16)

            sp.dma_start(adjt32[:, :, :], adj_t.rearrange("(t p) n -> p t n", p=P)).then_inc(adjt_loaded, 16)
            load(0, 0)
            load(0, 1)
            sp.dma_start(adj32, adj.rearrange("(t p) n -> p t n", p=P)).then_inc(adj_loaded, 16)
            load(0, 2)
            load(0, 3)
            with sp.Fori(0, GROUPS - 1) as g:
                for pair in PAIRS:
                    for b in pair:
                        reload(g, b)
                    for b in pair:
                        store(g, b)
            for b in range(SLOTS):
                store(GROUPS - 1, b)
            for b in range(SLOTS):
                sp.wait_ge(stored[b], 16 * GROUPS + PRIMED)

        @block.gpsimd
        def _(pool):
            pool.memset(half_neg[:, :], -0.5).then_inc(consts_set, 1)
            pool.memset(ones[:, :], 1.0).then_inc(consts_set, 1)
            pool.memset(ident[:, :], 0.0).then_inc(consts_set, 1)
            pool.memset(eps[:, :], EPS).then_inc(consts_set, 1)
            pool.wait_ge(consts_set, 4)
            pool.affine_select(out=ident[:, :], in_=ident[:, :], compare_op=ALU.not_equal, fill=1.0,
                               base=0, pattern=[[-1, P]], channel_multiplier=1).then_inc(consts_set, 1)

            def low_part(low, full, high, ready, n, done):
                pool.wait_ge(ready, n)
                pool.tensor_tensor(low, full, high.bitcast(F32), ALU.subtract).then_inc(done, 1)

            def fill(g, b):
                low_part(nodes_lo_t[:, b, :], x_in[:, b, :], nodes_hi_t[:, b, :],
                         nodes_hi[b], N_SPLIT * g + 1, nodes_lo[b])

            def late_phase(phase, g, k, b):
                if phase == "norm":
                    n = norm_count(g, k, b)
                    pool.wait_ge(var_done, n)
                    pool.tensor_tensor(rstd_t[:, b, :], var_t[:, b, :], half_neg[:, :], ALU.pow).then_inc(rstd_done, 1)
                    if k < 3:
                        low_part(nodes_lo_t[:, b, :], nodes32[:, b, :], nodes_hi_t[:, b, :],
                                 nodes_hi[b], N_SPLIT * g + STEPS + k + 1, nodes_lo[b])
                elif phase == "channels":
                    pool.wait_ge(chan_hi[b], N_CHAN * g + k + 1)
                    low_part(chan_lo_t[:, b, :], chan32[:, b, :], chan_hi_t[:, b, :],
                             chan_done[b], N_CHAN * g + k + 1, chan_lo[b])
                elif phase == "values":
                    low_part(nodes_lo_t[:, b, :], row32[:, b, :], nodes_hi_t[:, b, :],
                             hup_hi, SLOTS * g + b + 1, hup_lo)
                elif phase == "refill":
                    fill(g + 1, b)

            def stage(late, refill=True):
                for n in range(LAST_SPOT + 1):
                    for phase, g, k, b in late_spot(n, late):
                        if phase != "refill" or refill:
                            late_phase(phase, g, k, b)

            for b in range(SLOTS):
                fill(0, b)
            with pool.Fori(0, GROUPS - 1) as g:
                stage((g, PAIRS[0]))
                stage((g, PAIRS[1]))
            stage((GROUPS - 1, PAIRS[0]), refill=False)
            stage((GROUPS - 1, PAIRS[1]), refill=False)

        @block.scalar
        def _(act):
            act.dma_start(w_in[:, :, :], weights).then_inc(w_loaded, 16)
            act.dma_start(cols[:, :], columns).then_inc(cols_loaded, 16)
            act.dma_start(rows[:, :], row_in).then_inc(rows_loaded, 16)
            act.wait_ge(adjt_loaded, 16)
            act.activation(ap_hi[0][:, :, :], adjt32[:, :, :], ACT.Copy).then_inc(adjt_hi, 1)

            def fill(g, b):
                act.wait_ge(x_loaded[b], 16 * g + 16)
                act.activation(nodes_hi_t[:, b, :], x_in[:, b, :], ACT.Copy).then_inc(nodes_hi[b], 1)

            fill(0, 0)
            fill(0, 1)
            act.wait_ge(adj_loaded, 16)
            act.activation(chan_hi_t[:, :, :], adj32, ACT.Copy).then_inc(adjn_hi, 1)
            act.wait_ge(w_mixed, 1)
            act.activation(w_hi[:, :, :], mixed, ACT.Copy).then_inc(w_split, 1)
            fill(0, 2)
            fill(0, 3)

            def prepare(n):
                if n in POWER_SPOTS:
                    k, t = divmod(POWER_SPOTS.index(n), NT)
                    act.wait_ge(power_ready, NT * k + t + 1)
                    act.activation(ap_hi[k + 1][:, t, :], power_bank[t][:, :], ACT.Copy).then_inc(power_hi, 1)

            def neighbours(g, i, b):
                act.wait_ge(agg_ready[b], N_AGG * g + i // 2 + 1)
                act.activation(agg_hi_t[:, b, :], bank_a[b][:, :], ACT.Copy).then_inc(agg_hi[b], 1)

            def candidate(g, i, b):
                act.wait_ge(cand_ready, gated_count(g, i, b))
                act.activation(work[:, b, N:2 * N], bank_a[b][:, :], ACT.Tanh,
                               bias=bias_h[:, :]).then_inc(cand_done, 1)

            def reset_gate(g, i, b):
                act.wait_ge(rgate_ready, gated_count(g, i, b))
                act.wait_ge(stored[b], 16 * g + PRIMED)
                act.activation(nodes32[:, b, :], bank_b[b][:, :], ACT.Tanh,
                               bias=bias_r[:, :], scale=0.5).then_inc(r_done, 1)

            def turn_state(g, i, b):
                if i // 2 < STEPS - 1:
                    act.wait_ge(nodes_ready[b], N_NODES * g + i // 2 + 1)
                    act.activation(nodes_hi_t[:, b, :], bank_b[b][:, :], ACT.Copy).then_inc(nodes_hi[b], 1)

            def update_gate(g, i, b):
                act.wait_ge(zgate_ready, gated_count(g, i, b))
                act.activation(chan32[:, b, :], bank_b[b][:, :], ACT.Tanh,
                               bias=bias_z[:, :], scale=0.5).then_inc(z_done, 1)

            def late_agg(b, n):
                act.wait_ge(agg_ready[b], n)
                act.activation(agg_hi_t[:, b, :], bank_b[b][:, :], ACT.Copy).then_inc(agg_hi[b], 1)

            def late_phase(phase, g, k, b):
                n = SLOTS * g + b + 1
                if phase == "norm" and k < 3:
                    act.wait_ge(normed[b], N_LN * g + k + 1 + PRIMED)
                    act.activation(nodes_hi_t[:, b, :], nodes32[:, b, :], ACT.Copy).then_inc(nodes_hi[b], 1)
                elif phase == "channels":
                    act.wait_ge(chan_ready[b], N_CHAN * g + k + 1)
                    act.activation(chan32[:, b, :], bank_a[b][:, :], ACT.Copy,
                                   accum_out=xsum_t[:, b, :]).then_inc(chan_done[b], 1)
                    act.activation(chan_hi_t[:, b, :], bank_a[b][:, :], ACT.Copy).then_inc(chan_hi[b], 1)
                elif phase == "agg":
                    late_agg(b, N_AGG * g + STEPS + k)
                elif phase == "power" and k < 3:
                    late_agg(b, N_AGG * g + STEPS + 2 + k)
                elif phase == "cols":
                    act.wait_ge(cols_ready, n)
                    act.activation(srow_t[:, b, :], bank_b[b][0:1, 0:P], ACT.Copy).then_inc(srow_done, 1)
                elif phase == "rank1":
                    act.wait_ge(rank_ready, n)
                    act.activation(rank_hi_t[:, b, :], bank_b[b][:, 2 * P:3 * P], ACT.Copy).then_inc(rank_hi, 1)
                elif phase == "rows":
                    act.wait_ge(vrow_ready, n)
                    act.activation(row32[:, b, :], bank_b[b][:, :], ACT.Copy, scale=LEAK).then_inc(vleak_done, 1)
                elif phase == "weights":
                    act.wait_ge(nmax_done, n)
                    for t in range(NT):
                        e = work[:, b, t * HALF:(t + 1) * HALF]
                        ins = act.activation(e, e, ACT.Exp, bias=nmax_t[:, b, t:t + 1],
                                             accum_out=lsum_t[:, b, t:t + 1])
                    ins.then_inc(low_done, 1)
                    act.wait_ge(udif_done, n)
                    act.activation(uexp_t[:, b, :], udif_t[:, b, :], ACT.Exp).then_inc(up_done, 1)
                elif phase == "values":
                    act.wait_ge(hup_done, n)
                    act.activation(nodes_hi_t[:, b, :], row32[:, b, :], ACT.Copy).then_inc(hup_hi, 1)
                elif phase == "refill":
                    act.wait_ge(out_ready[b], N_OUT * g + N_OUT)
                    fill(g + 1, b)

            def late_spot_phases(n, late, refill, slow):
                for phase, g, k, b in late_spot(n, late):
                    if (phase in ("norm", "weights")) == slow and (phase != "refill" or refill):
                        late_phase(phase, g, k, b)

            def stage(gated, late, refill=True, preparing=False):
                for i, now, before in turns(gated, late):
                    if now:
                        neighbours(*now)
                    if before:
                        candidate(*before)
                    if i:
                        late_spot_phases(2 * i - 1, late, refill, slow=True)
                    if preparing:
                        prepare(2 * i)
                    late_spot_phases(2 * i, late, refill, slow=False)
                    if now:
                        reset_gate(*now)
                    if before:
                        turn_state(*before)
                    if now:
                        update_gate(*now)
                    late_spot_phases(2 * i, late, refill, slow=True)
                    if preparing:
                        prepare(2 * i + 1)
                    late_spot_phases(2 * i + 1, late, refill, slow=False)
                late_spot_phases(LAST_SPOT, late, refill, slow=True)

            first, second = PAIRS
            stage((0, first), None, preparing=True)
            with act.Fori(0, GROUPS - 1) as g:
                stage((g, second), (g, first))
                stage((g + 1, first), (g, second))
            stage((GROUPS - 1, second), (GROUPS - 1, first), refill=False)
            stage(None, (GROUPS - 1, second), refill=False)

        @block.vector
        def _(dve):
            dve.wait_ge(adjt_hi, 1)
            dve.tensor_tensor(ap_lo[0][:, :, :], adjt32[:, :, :], ap_hi[0][:, :, :].bitcast(F32),
                              ALU.subtract).then_inc(adjt_lo, 1)
            dve.wait_ge(w_loaded, 16)
            dve.wait_ge(cols_loaded, 16)
            dve.wait_ge(prep_small, 1)
            dve.wait_ge(consts_set, 5)
            dve.tensor_copy(wrgb[:, :], bank_b[0][:, 0:2]).then_inc(prep_small_read, 1)
            dve.tensor_copy(wo_att[:, 0:2], bank_b[1][:, 0:2]).then_inc(prep_small_read, 1)
            dve.wait_ge(prep_small_read, 2)
            dve.tensor_tensor(wo_att[:, 2:3], wo_att[:, 0:1], wo_att[:, 1:2], ALU.add).then_inc(prep_small_read, 1)
            dve.tensor_tensor(mixed[:, S_R, :], w_in[:, W4A, :], w_in[:, W4B, :], ALU.add).then_inc(prep_small_read, 1)
            dve.tensor_tensor(mixed[:, S_H, :], w_in[:, W5A, :], w_in[:, W5B, :], ALU.add)
            dve.tensor_tensor(mixed[:, S_ZR, :], w_in[:, W3A, :], w_in[:, W3B, :], ALU.add).then_inc(prep_small_read, 1)
            dve.tensor_copy(mixed[:, S_U3:S_U5 + 1, :], w_in[:, U3:U5 + 1, :])
            dve.tensor_scalar(mixed[:, S_W1, :], w_in[:, W1, :], wrgb[:, 0:1], None, ALU.mult)
            dve.tensor_copy(mixed[:, S_X0, :], w_in[:, C0, :])
            dve.tensor_tensor(mixed[:, S_X1:S_X3 + 1, :], w_in[:, C1:C3 + 1, :], w_in[:, C4:C6 + 1, :], ALU.add)
            dve.tensor_copy(mixed[:, S_WO:S_WS + 1, :], w_in[:, WO:WS + 1, :])
            dve.tensor_scalar(mixed[:, S_SJ, :], ones[:, :], cols[:, WJ:WJ + 1], None, ALU.mult)
            dve.wait_ge(prep_small_read, 3)
            dve.tensor_scalar(mixed[:, S_V, :], ones[:, :], wo_att[:, 2:3], None, ALU.mult)
            dve.tensor_scalar(mixed[:, S_P1, :], ones[:, :], wo_att[:, 0:1], None, ALU.mult)
            dve.tensor_scalar(mixed[:, S_P2, :], ones[:, :], wo_att[:, 1:2], None, ALU.mult)
            dve.tensor_tensor(bias_in[:, 0:1], cols[:, B4:B4 + 1], cols[:, BU3:BU3 + 1], ALU.add).then_inc(bias_sum, 1)
            dve.tensor_tensor(bias_in[:, 1:2], cols[:, B3:B3 + 1], cols[:, BU3:BU3 + 1], ALU.add).then_inc(bias_sum, 1)
            dve.wait_ge(bias_sum, 2)
            dve.tensor_scalar(bias_r[:, :], bias_in[:, 0:1], 0.5, None, ALU.mult)
            dve.tensor_scalar(bias_z[:, :], bias_in[:, 1:2], 0.5, None, ALU.mult)
            dve.tensor_scalar(u5_half[:, :], w_in[:, U5, :], 0.5, None, ALU.mult)
            dve.tensor_tensor(bias_h[:, :], cols[:, B5:B5 + 1], cols[:, BU5:BU5 + 1], ALU.add)
            dve.wait_ge(prep_small_read, 5)
            dve.tensor_tensor(mixed[:, S_ZR, :], mixed[:, S_ZR, :], mixed[:, S_R, :], ALU.subtract).then_inc(w_mixed, 1)
            dve.wait_ge(w_split, 1)
            dve.tensor_tensor(w_lo[:, :, :], mixed, w_hi[:, :, :].bitcast(F32), ALU.subtract).then_inc(w_split, 1)
            dve.wait_ge(adjn_hi, 1)
            dve.tensor_tensor(chan_lo_t[:, :, :], adj32, chan_hi_t[:, :, :].bitcast(F32),
                              ALU.subtract).then_inc(adjn_lo, 1)

            def masks():
                dve.wait_ge(w_split, 2)
                dve.tensor_scalar(low_neg[:, :, :], adjt32[:, :, 0:HALF], 0.0, -NEG_BIG, ALU.is_gt, ALU.mult).then_inc(masks_set, 1)
                dve.tensor_scalar(up32, adjt32[:, :, HALF:N], 0.0, None, ALU.is_gt).then_inc(masks_set, 1)
                dve.wait_ge(masks_set, 2)
                dve.tensor_scalar(low_neg[:, :, :], low_neg[:, :, :], NEG_BIG, None, ALU.add).then_inc(masks_set, 1)
                dve.tensor_reduce(any_up[:, :], up32, AX_X, ALU.max).then_inc(masks_set, 1)
                dve.wait_ge(masks_set, 4)
                dve.tensor_scalar(no_up[:, :], any_up[:, :], -1.0, 1.0, ALU.mult, ALU.add).then_inc(masks_set, 1)
                dve.wait_ge(masks_set, 5)
                dve.tensor_scalar(up_neg[:, :], no_up[:, :], NEG_BIG, None, ALU.mult)
                for t in range(NT):
                    dve.tensor_scalar(up_mask[:, t, :], up32[:, t, :], no_up[:, t:t + 1], None, ALU.max).then_inc(masks_set, 1)
                dve.wait_ge(masks_set, 5 + NT)
                dve.tensor_reduce(up_count[:, :], up_mask[:, :, :].bitcast(F32), AX_X, ALU.add).then_inc(masks_set, 1)
                dve.wait_ge(masks_set, 6 + NT)

            def prepare(n):
                if n in POWER_SPOTS:
                    k, t = divmod(POWER_SPOTS.index(n), NT)
                    dve.wait_ge(power_hi, NT * k + t + 1)
                    dve.tensor_tensor(ap_lo[k + 1][:, t, :], power_bank[t][:, :],
                                      ap_hi[k + 1][:, t, :].bitcast(F32), ALU.subtract).then_inc(power_lo, 1)
                elif n == MASK_SPOT:
                    masks()

            def agg_low(b, n, bank):
                dve.wait_ge(agg_hi[b], n)
                dve.tensor_tensor(agg_lo_t[:, b, :], bank[b][:, :], agg_hi_t[:, b, :].bitcast(F32),
                                  ALU.subtract).then_inc(agg_lo[b], 1)

            def neighbours(g, i, b):
                agg_low(b, N_AGG * g + i // 2 + 1, bank_a)

            def reset_gate(g, i, b):
                dve.wait_ge(h_loaded[b], 16 * g + 16)
                dve.wait_ge(r_done, gated_count(g, i, b))
                dve.scalar_tensor_tensor(out=work[:, b, 0:N], in0=nodes32[:, b, :], scalar=1.0,
                                         in1=h_ch[:, b, :], op0=ALU.add, op1=ALU.mult).then_inc(rh_done, 1)

            def turn_state(g, i, b):
                if i // 2 < STEPS - 1:
                    dve.wait_ge(nodes_hi[b], N_SPLIT * g + i // 2 + 2)
                    dve.tensor_tensor(nodes_lo_t[:, b, :], bank_b[b][:, :], nodes_hi_t[:, b, :].bitcast(F32),
                                      ALU.subtract).then_inc(nodes_lo[b], 1)

            def candidate(g, i, b):
                n = gated_count(g, i, b)
                cand = work[:, b, N:2 * N]
                dve.wait_ge(cand_done, n)
                dve.tensor_tensor(cand, cand, h_ch[:, b, :], ALU.subtract).then_inc(delta_done, 1)
                dve.wait_ge(z_done, n)
                dve.wait_ge(delta_done, n)
                dve.scalar_tensor_tensor(out=cand, in0=chan32[:, b, :], scalar=1.0, in1=cand,
                                         op0=ALU.add, op1=ALU.mult).then_inc(gated_done, 1)
                dve.wait_ge(gated_done, n)
                dve.scalar_tensor_tensor(out=h_ch[:, b, :], in0=cand, scalar=0.5, in1=h_ch[:, b, :],
                                         op0=ALU.mult, op1=ALU.add).then_inc(h_done[b], 1)

            def norm(g, k, b):
                n = N_LN * g + k + 1
                if k == 0:
                    dve.wait_ge(nodes_ready[b], N_NODES * g + STEPS)
                    dve.tensor_tensor(nodes32[:, b, :], bank_b[b][:, :], x_in[:, b, :], ALU.add).then_inc(first_sum, 1)
                    dve.wait_ge(first_sum, SLOTS * g + b + 1)
                    y = nodes32[:, b, :]
                else:
                    dve.wait_ge(nodes_ready[b], N_NODES * g + STEPS + k)
                    y = bank_b[b][:, :]
                for t in range(NT):
                    dve.bn_stats(stats_t[:, b, t, :], y[:, t * P:(t + 1) * P])
                dve.drain()
                for t in range(NT):
                    ins = dve.bn_aggr(moments_t[:, b, t, :], stats_t[:, b, t, :])
                ins.then_inc(moments_done, 1)
                dve.wait_ge(moments_done, norm_count(g, k, b))
                dve.tensor_tensor(var_t[:, b, :], moments_t[:, b, :, 1], eps[:, :], ALU.add).then_inc(var_done, 1)

            def apply_norm(g, k, b):
                y = bank_b[b] if k else nodes32[:, b, :]
                dve.wait_ge(rstd_done, norm_count(g, k, b))
                for t in range(NT):
                    ins = dve.tensor_scalar(nodes32[:, b, t * P:(t + 1) * P], y[:, t * P:(t + 1) * P],
                                            moments_t[:, b, t, 0:1], rstd_t[:, b, t:t + 1],
                                            ALU.subtract, ALU.mult)
                ins.then_inc(normed[b], 1)

            def relation_sums(g, b):
                n = SLOTS * g + b + 1
                dve.wait_ge(sj_ready, n)
                dve.wait_ge(chan_done[b], N_CHAN * g + 1)
                dve.tensor_tensor_reduce(trash[:, :], bank_a[b][:, :], chan32[:, b, :], 1.0, 0.0,
                                         ALU.mult, ALU.add, tcol_t[:, b, :]).then_inc(t_done, 1)
                dve.wait_ge(t_done, n)
                dve.scalar_tensor_tensor(out=mix_t[:, b, :], in0=xsum_t[:, b, :], scalar=wrgb[:, 1:2],
                                         in1=tcol_t[:, b, :], op0=ALU.mult, op1=ALU.add).then_inc(mix_done, 1)

            def residual(g, k, b, bank, scalar):
                dve.wait_ge(out_ready[b], N_OUT * g + k)
                dve.scalar_tensor_tensor(out=row32[:, b, :], in0=bank[b][:, :], scalar=scalar,
                                         in1=chan32[:, b, :], op0=ALU.add, op1=ALU.add).then_inc(resid_done[b], 1)

            def logits(g, b):
                n = SLOTS * g + b + 1
                dve.wait_ge(vleak_done, n)
                dve.tensor_tensor(row32[:, b, :], bank_b[b][:, :], row32[:, b, :], ALU.max).then_inc(vrow_done, 1)
                dve.wait_ge(pair_ready, n)
                for c in range(2):
                    if c:
                        dve.wait_ge(pair_done, 2 * n - 1)
                    dve.tensor_tensor_reduce(trash[:, 0:P], bank_a[b][:, c * P:(c + 1) * P], ident[:, :], 1.0, 0.0,
                                             ALU.mult, ALU.add, pair_t[:, b, c:c + 1]).then_inc(pair_done, 1)
                dve.wait_ge(pair_done, 2 * n)
                dve.scalar_tensor_tensor(out=pairl_t[:, b, :], in0=pair_t[:, b, :], scalar=LEAK,
                                         in1=pair_t[:, b, :], op0=ALU.mult, op1=ALU.max).then_inc(pairl_done, 1)

            def maxima(g, b):
                n = SLOTS * g + b + 1
                dve.wait_ge(vrow_done, n)
                dve.wait_ge(pairl_done, n)
                for c in range(2):
                    ins = dve.tensor_tensor(umax_t[:, b, 2 * c:2 * c + 2], pairl_t[:, b, :],
                                            up_neg[:, 2 * c:2 * c + 2], ALU.add)
                ins.then_inc(umax_done, 1)
                for t in range(NT):
                    ins = dve.tensor_tensor_reduce(work[:, b, t * HALF:(t + 1) * HALF],
                                                   row32[:, b, t // 2:N:2], low_neg[:, t, :], 1.0, 3 * NEG_BIG,
                                                   ALU.add, ALU.max, lmax_t[:, b, t:t + 1])
                ins.then_inc(lmax_done, 1)
                dve.wait_ge(lmax_done, n)
                dve.wait_ge(umax_done, n)
                dve.tensor_tensor(lmax_t[:, b, :], lmax_t[:, b, :], umax_t[:, b, :], ALU.max).then_inc(lmax2_done, 1)
                dve.wait_ge(lmax2_done, n)
                dve.tensor_scalar(nmax_t[:, b, :], lmax_t[:, b, :], -1.0, None, ALU.mult).then_inc(nmax_done, 1)
                dve.tensor_tensor(udif_t[:, b, :], umax_t[:, b, :], lmax_t[:, b, :], ALU.subtract).then_inc(udif_done, 1)

            def values(g, b):
                n = SLOTS * g + b + 1
                dve.wait_ge(up_done, n)
                dve.tensor_tensor(usum_t[:, b, :], uexp_t[:, b, :], up_count[:, :], ALU.mult).then_inc(usum_done, 1)
                dve.wait_ge(usum_done, n)
                dve.wait_ge(low_done, n)
                dve.tensor_tensor(den_t[:, b, :], usum_t[:, b, :], lsum_t[:, b, :], ALU.add).then_inc(den_done, 1)
                dve.wait_ge(den_done, n)
                dve.reciprocal(rden_t[:, b, :], den_t[:, b, :]).then_inc(rden_done, 1)
                dve.wait_ge(rden_done, n)
                dve.tensor_tensor(uden_t[:, b, :], uexp_t[:, b, :], rden_t[:, b, :], ALU.mult).then_inc(uden_done, 1)
                dve.wait_ge(att_ready, n)
                dve.wait_ge(uden_done, n)
                h = bank_a[b][:, :].rearrange("p (t c) -> p t c", t=NT)
                dve.tensor_tensor(row32[:, b, :].rearrange("p (t c) -> p t c", t=NT), h,
                                  uden_t[:, b, :].unsqueeze(2).to_broadcast([P, NT, P]), ALU.mult).then_inc(hup_done, 1)
                dve.tensor_tensor(nodes32[:, b, :].rearrange("p (t c) -> p t c", t=NT), h,
                                  rden_t[:, b, :].unsqueeze(2).to_broadcast([P, NT, P]), ALU.mult).then_inc(hlow_done, 1)

            def late_phase(phase, g, k, b):
                n = SLOTS * g + b + 1
                if phase == "norm":
                    norm(g, k, b)
                elif phase == "agg":
                    agg_low(b, N_AGG * g + STEPS + k, bank_b)
                elif phase == "power" and k < 3:
                    agg_low(b, N_AGG * g + STEPS + 2 + k, bank_b)
                elif phase == "power":
                    residual(g, 2, b, bank_a, 0.0)
                elif phase == "sj":
                    relation_sums(g, b)
                elif phase == "cols":
                    dve.wait_ge(srow_done, n)
                    dve.tensor_tensor(ccol_t[:, b, :], bank_b[b][:, P:P + 1], cols[:, BIAS1:BIAS1 + 1],
                                      ALU.add).then_inc(ccol_done, 1)
                elif phase == "rank1":
                    dve.wait_ge(rank_hi, n)
                    dve.tensor_tensor(rank_lo_t[:, b, :], bank_b[b][:, 2 * P:3 * P],
                                      rank_hi_t[:, b, :].bitcast(F32), ALU.subtract).then_inc(rank_lo, 1)
                elif phase == "out1":
                    dve.wait_ge(ccol_done, n)
                    residual(g, 1, b, bank_a, ccol_t[:, b, :])
                elif phase == "rows":
                    logits(g, b)
                elif phase == "weights":
                    maxima(g, b)
                elif phase == "values":
                    values(g, b)
                elif phase == "attend":
                    residual(g, 3, b, bank_b, 0.0)

            def late_spot_phases(n, late, preparing):
                if preparing:
                    prepare(n)
                for phase, g, k, b in late_spot(n, late):
                    late_phase(phase, g, k, b)

            def late_spot_ends(n, late):
                for phase, g, k, b in late_spot(n, late):
                    if phase == "norm":
                        apply_norm(g, k, b)

            def stage(gated, late, preparing=False):
                for i, now, before in turns(gated, late):
                    if now:
                        neighbours(*now)
                    if i:
                        late_spot_ends(2 * i - 1, late)
                    if before:
                        candidate(*before)
                    late_spot_phases(2 * i, late, preparing)
                    if now:
                        reset_gate(*now)
                    late_spot_ends(2 * i, late)
                    if before:
                        turn_state(*before)
                    late_spot_phases(2 * i + 1, late, preparing)
                late_spot_ends(LAST_SPOT, late)

            first, second = PAIRS
            stage((0, first), None, preparing=True)
            with dve.Fori(0, GROUPS - 1) as g:
                stage((g, second), (g, first))
                stage((g + 1, first), (g, second))
            stage((GROUPS - 1, second), (GROUPS - 1, first))
            stage(None, (GROUPS - 1, second))

        @block.tensor
        def _(pe):
            def split_product(psum, lhs, rhs, start, stop):
                pe.matmul(psum, lhs[0], rhs[0], start=start, stop=False)
                pe.matmul(psum, lhs[0], rhs[1], start=False, stop=False)
                return pe.matmul(psum, lhs[1], rhs[0], start=False, stop=stop)

            def weight(n):
                return w_hi[:, n, :], w_lo[:, n, :]

            def tile_of(hi, lo, b, t):
                return hi[:, b, t * P:(t + 1) * P], lo[:, b, t * P:(t + 1) * P]

            def neighbour_sum(b, k, psum):
                for t in range(NT):
                    ins = split_product(psum, tile_of(nodes_hi_t, nodes_lo_t, b, t),
                                        (ap_hi[k - 1][:, t, :], ap_lo[k - 1][:, t, :]), t == 0, t == NT - 1)
                ins.then_inc(agg_ready[b], 1)

            def turn(psum, source):
                for t in range(NT):
                    ins = pe.transpose(psum[:, t * P:(t + 1) * P], source[:, t * P:(t + 1) * P], ident[:, :])
                return ins

            pe.wait_ge(consts_set, 5)
            pe.wait_ge(rows_loaded, 16)
            pe.matmul(bank_b[0][:, 0:2], ones[0:1, :], rows[:, P:P + 2], start=True, stop=True)
            pe.wait_ge(w_loaded, 16)
            pe.wait_ge(cols_loaded, 16)
            pe.matmul(bank_b[1][:, 0:2], w_in[:, WOT, :], cols[:, A1:A2 + 1], start=True, stop=True).then_inc(prep_small, 1)

            def prepare(n):
                if n in POWER_SPOTS:
                    k, m = divmod(POWER_SPOTS.index(n), NT)
                    if m == 0:
                        if k == 0:
                            pe.wait_ge(adjn_lo, 1)
                        else:
                            pe.wait_ge(power_lo, NT)
                    for t in range(NT):
                        ins = split_product(power_bank[m][:, :], tile_of(chan_hi_t, chan_lo_t, t, m),
                                            (ap_hi[k][:, t, :], ap_lo[k][:, t, :]), t == 0, t == NT - 1)
                    ins.then_inc(power_ready, 1)
                elif n == LAST_SPOT:
                    pe.wait_ge(power_lo, 2 * NT)
                    pe.wait_ge(masks_set, 6 + NT)

            def neighbours(g, i, b):
                pe.wait_ge(nodes_lo[b], N_SPLIT * g + i // 2 + 1)
                neighbour_sum(b, 1, bank_a[b][:, :])

            def candidate(g, i, b):
                pe.wait_ge(rh_done, gated_count(g, i, b))
                pe.matmul(bank_a[b][:, :], u5_half[:, :], work[:, b, 0:N],
                          start=False, stop=True).then_inc(cand_ready, 1)

            def reset_gate(g, i, b):
                pe.wait_ge(agg_lo[b], N_AGG * g + i // 2 + 1)
                pe.wait_ge(h_loaded[b], 16 * g + 16)
                pe.wait_ge(normed[b], N_LN * g + PRIMED)
                agg = (agg_hi_t[:, b, :], agg_lo_t[:, b, :])
                split_product(bank_b[b][:, :], weight(S_R), agg, True, False)
                pe.matmul(bank_b[b][:, :], w_in[:, U3, :], h_ch[:, b, :], start=False,
                          stop=True).then_inc(rgate_ready, 1)
                split_product(bank_a[b][:, :], weight(S_H), agg, True, False)

            def turn_state(g, i, b):
                pe.wait_ge(h_done[b], STEPS * g + i // 2 + 1)
                turn(bank_b[b], h_ch[:, b, :]).then_inc(nodes_ready[b], 1)

            def update_gate(g, i, b):
                pe.wait_ge(r_done, gated_count(g, i, b))
                for w, a, last in ((w_hi, agg_hi_t, False), (w_hi, agg_lo_t, False), (w_lo, agg_hi_t, True)):
                    ins = pe.matmul(bank_b[b][:, :], w[:, S_ZR, :], a[:, b, :], start=False, stop=last,
                                    skip_group_check=True)
                ins.then_inc(zgate_ready, 1)

            def power(g, k, b):
                pe.wait_ge(agg_lo[b], N_AGG * g + STEPS + 1 + k)
                if k == 1:
                    pe.wait_ge(chan_lo[b], N_CHAN * g + 2)
                    pe.wait_ge(chan_done[b], N_CHAN * g + 2)
                    split_product(bank_a[b][:, :], weight(S_X0), (chan_hi_t[:, b, :], chan_lo_t[:, b, :]), True, False)
                ins = split_product(bank_a[b][:, :], weight(S_X0 + k), (agg_hi_t[:, b, :], agg_lo_t[:, b, :]), False, k == 3)
                if k == 3:
                    ins.then_inc(out_ready[b], 1)
                else:
                    neighbour_sum(b, k + 1, bank_b[b][:, :])

            def att_rows(g, b):
                x = (chan_hi_t[:, b, :], chan_lo_t[:, b, :])
                even = tuple(v[:, 0:N:2] for v in x)
                odd = tuple(v[:, 1:N:2] for v in x)
                pe.wait_ge(chan_lo[b], N_CHAN * g + 3)
                pe.wait_ge(chan_done[b], N_CHAN * g + 3)
                split_product(bank_b[b][:, :], weight(S_V), x, True, True).then_inc(vrow_ready, 1)
                split_product(bank_a[b][:, 0:HALF], weight(S_P1), even, True, False)
                split_product(bank_a[b][:, 0:HALF], weight(S_P2), odd, False, True).then_inc(pair_ready, 1)

            def att_values(g, b):
                pe.wait_ge(pair_done, 2 * (SLOTS * g + b + 1))
                for t in range(NT):
                    ins = split_product(bank_a[b][:, t * P:(t + 1) * P], tile_of(chan_hi_t, chan_lo_t, b, t),
                                        weight(S_WO), True, True)
                ins.then_inc(att_ready, 1)
                pe.wait_ge(vrow_done, SLOTS * g + b + 1)
                split_product(bank_b[b][:, :], weight(S_WS), (chan_hi_t[:, b, :], chan_lo_t[:, b, :]), True, False)

            def attend(g, b):
                n = SLOTS * g + b + 1
                pe.wait_ge(hlow_done, n)
                for t in range(NT):
                    pe.matmul(bank_b[b][:, 0:HALF], nodes32[:, b, t * P:(t + 1) * P],
                              work[:, b, t * HALF:(t + 1) * HALF], start=False, stop=False)
                pe.wait_ge(hup_lo, n)
                for t in range(NT):
                    hi, lo = tile_of(nodes_hi_t, nodes_lo_t, b, t)
                    pe.matmul(bank_b[b][:, HALF:N], hi, up_mask[:, t, :], start=False, stop=False)
                    ins = pe.matmul(bank_b[b][:, HALF:N], lo, up_mask[:, t, :], start=False, stop=(t == NT - 1))
                ins.then_inc(out_ready[b], 1)

            def late_phase(phase, g, k, b):
                n = SLOTS * g + b + 1
                if phase == "channels":
                    pe.wait_ge(normed[b], N_LN * g + k + 1 + PRIMED)
                    turn(bank_a[b], nodes32[:, b, :]).then_inc(chan_ready[b], 1)
                elif phase == "turn":
                    pe.wait_ge(resid_done[b], N_OUT * g + k)
                    turn(bank_b[b], row32[:, b, :]).then_inc(nodes_ready[b], 1)
                elif phase == "agg":
                    pe.wait_ge(nodes_lo[b], N_SPLIT * g + STEPS + k)
                    neighbour_sum(b, 1, bank_b[b][:, :])
                elif phase == "sj":
                    pe.wait_ge(chan_lo[b], N_CHAN * g + 1)
                    split_product(bank_a[b][:, :], weight(S_SJ), (chan_hi_t[:, b, :], chan_lo_t[:, b, :]),
                                  True, True).then_inc(sj_ready, 1)
                elif phase == "cols":
                    pe.wait_ge(agg_lo[b], N_AGG * g + STEPS + 1)
                    pe.wait_ge(mix_done, n)
                    pe.matmul(bank_b[b][0:1, 0:P], xsum_t[:, b, :], w_in[:, W1, :], start=True, stop=True)
                    pe.matmul(bank_b[b][:, P:P + 1], w_in[:, W1, :], mix_t[:, b, :], start=True,
                              stop=True).then_inc(cols_ready, 1)
                elif phase == "rank1":
                    pe.wait_ge(srow_done, n)
                    pe.wait_ge(ccol_done, n)
                    pe.matmul(bank_b[b][:, 2 * P:3 * P], rows[:, 0:P], srow_t[:, b, :], start=True,
                              stop=True).then_inc(rank_ready, 1)
                elif phase == "out1":
                    pe.wait_ge(rank_lo, n)
                    split_product(bank_a[b][:, :], weight(S_W1), (agg_hi_t[:, b, :], agg_lo_t[:, b, :]), True, False)
                    split_product(bank_a[b][:, :], (rank_hi_t[:, b, :], rank_lo_t[:, b, :]),
                                  (chan_hi_t[:, b, :], chan_lo_t[:, b, :]), False, True).then_inc(out_ready[b], 1)
                elif phase == "power":
                    power(g, k, b)
                elif phase == "rows":
                    att_rows(g, b)
                elif phase == "weights":
                    att_values(g, b)
                elif phase == "attend":
                    attend(g, b)

            def late_spot_phases(n, late, preparing):
                if preparing:
                    prepare(n)
                for phase, g, k, b in late_spot(n, late):
                    late_phase(phase, g, k, b)

            def stage(gated, late, preparing=False):
                for i, now, before in turns(gated, late):
                    if now:
                        neighbours(*now)
                    if before:
                        candidate(*before)
                    late_spot_phases(2 * i, late, preparing)
                    if now:
                        if preparing and i == 0:
                            pe.wait_ge(w_split, 2)
                        reset_gate(*now)
                    if before:
                        turn_state(*before)
                    if now:
                        update_gate(*now)
                    late_spot_phases(2 * i + 1, late, preparing)

            pe.wait_ge(adjt_lo, 1)
            first, second = PAIRS
            stage((0, first), None, preparing=True)
            with pe.Fori(0, GROUPS - 1) as g:
                stage((g, second), (g, first))
                stage((g + 1, first), (g, second))
            stage((GROUPS - 1, second), (GROUPS - 1, first))
            stage(None, (GROUPS - 1, second))


def kernel(x, adj, L0_gnn_w3_w, L0_gnn_w3_b, L0_gnn_u3_w, L0_gnn_u3_b, L0_gnn_w4_w, L0_gnn_w4_b, L0_gnn_w5_w,
           L0_gnn_w5_b, L0_gnn_u5_w, L0_gnn_u5_b, L1_gnn_g_w, L1_gnn_g_b, L1_gnn_weight, L1_gnn_bias,
           L2_gnn_weight_1, L3_gnn_others_weight, L3_gnn_self_weight, L3_gnn_att_weight):
    import numpy as np
    import concourse.bacc as bacc
    from concourse.bass_utils import run_bass_kernel_spmd

    def halves(w):
        w = np.asarray(w)
        return [w[:, :P].T, w[:, P:].T]

    stacked = [*halves(L0_gnn_w3_w), *halves(L0_gnn_w4_w), *halves(L0_gnn_w5_w),
               np.asarray(L0_gnn_u3_w).T, np.asarray(L0_gnn_u5_w).T, np.asarray(L1_gnn_weight),
               *[np.asarray(L2_gnn_weight_1)[:, :, k] for k in range(7)],
               np.asarray(L3_gnn_others_weight), np.asarray(L3_gnn_self_weight), np.asarray(L3_gnn_others_weight).T]
    g_w = np.asarray(L1_gnn_g_w)
    att = np.asarray(L3_gnn_att_weight)[:, 0]
    columns = [np.asarray(v) for v in (L0_gnn_w3_b, L0_gnn_w4_b, L0_gnn_w5_b, L0_gnn_u3_b, L0_gnn_u5_b)]
    columns += [g_w[:P], np.asarray(L1_gnn_bias), att[:P], att[P:]]
    row = np.concatenate([g_w[P:], np.asarray(L1_gnn_g_b).reshape(1)])[None, :]
    arrays = {
        "x_nodes": np.ascontiguousarray(x),
        "x_channels": np.ascontiguousarray(np.asarray(x).transpose(0, 2, 1)),
        "adj": np.ascontiguousarray(adj),
        "adj_t": np.ascontiguousarray(np.asarray(adj).T),
        "weights": np.ascontiguousarray(np.stack(stacked, axis=1)),
        "columns": np.ascontiguousarray(np.stack(columns, axis=1)),
        "row_in": np.ascontiguousarray(row),
    }
    nc = bacc.Bacc("TRN2", target_bir_lowering=False, num_devices=1)
    args = [nc.dram_tensor(name, a.shape, mybir.dt.from_np(a.dtype), kind="ExternalInput").ap()
            for name, a in arrays.items()]
    out = nc.dram_tensor("out", (BATCH, N, P), F32, kind="ExternalOutput").ap()
    build(nc, *args, out)
    result = run_bass_kernel_spmd(nc, [arrays], core_ids=[0])
    return result.results[0]["out"]
```

```python
from contextlib import ExitStack

import concourse.bass as bass
from concourse import mybir

F32 = mybir.dt.float32
F32R = mybir.dt.float32r
ALU = mybir.AluOpType
ACT = mybir.ActivationFunctionType
AX_X = mybir.AxisListType.X

P = 128
N = 512
NT = N // P
HALF = N // 2
BATCH = 32
SLOTS = 4
GROUPS = BATCH // SLOTS
STEPS = 5
EPS = 1e-5
NEG_BIG = -9000000000000000.0
LEAK = 0.1

(W3A, W3B, W4A, W4B, W5A, W5B, U3, U5, W1, C0, C1, C2, C3, C4, C5, C6, WO, WS, WOT) = range(19)
(B3, B4, B5, BU3, BU5, WJ, BIAS1, A1, A2) = range(9)
(S_R, S_H, S_ZR, S_U3, S_U5, S_W1, S_X0, S_X1, S_X2, S_X3, S_WO, S_WS, S_SJ, S_V, S_P1, S_P2) = range(16)
W_PARTS = (slice(S_R, S_U5 + 1), slice(S_U5 + 1, S_P2 + 1))

N_AGG = STEPS + 1 + 3
N_NODES = STEPS + 3
N_SPLIT = STEPS + 3
N_LN = 4
N_CHAN = 3
N_OUT = 3


PAIRS = ((0, 1), (2, 3))
TURNS = 2 * STEPS

PRIMED = 1


def gated_count(g, i, b):
    return SLOTS * STEPS * g + TURNS * (b // 2) + i + 1


def state_count(g, i):
    return TURNS * g + i + 1


PIECES = 5
STAGE = PIECES * TURNS
PE, SCALAR, VECTOR, POOL = range(2, 6)
LATE = (
    ("norm",     0, None    , None    , (2, 6)  , (4, 6) ),
    ("apply",    0, None    , (6, 11) , (4, 9)  , (4, 9) ),
    ("channels", 0, (7, 12) , (6, 11) , None    , (5, 12)),
    ("agg",      1, (7, 12) , (7, 12) , (11, 13), None   ),
    ("sj",       1, (8, 13) , None    , (11, 14), None   ),
    ("cols",     1, (14, 17), (14, 17), (13, 17), None   ),
    ("out1",     1, (16, 18), None    , (16, 17), None   ),
    ("turn",     1, (18, 19), None    , None    , None   ),
    ("norm",     1, None    , None    , (17, 20), (19, 21)),
    ("apply",    1, None    , (21, 23), (19, 21), (19, 24)),
    ("channels", 1, (22, 24), (22, 25), None    , (25, 26)),
    ("agg",      2, (22, 26), (26, 26), (25, 26), None   ),
    ("power",    1, (27, 29), (27, 28), (28, 29), None   ),
    ("power",    2, (30, 31), (31, 31), (31, 31), None   ),
    ("power",    3, (32, 33), None    , (32, 32), None   ),
    ("turn",     2, (33, 34), None    , None    , None   ),
    ("norm",     2, None    , None    , (32, 34), (34, 34)),
    ("apply",    2, None    , (36, 38), (34, 36), (37, 39)),
    ("channels", 2, (36, 39), (36, 39), None    , (37, 39)),
    ("rows",     3, (38, 42), (37, 43), (37, 43), None   ),
    ("weights",  3, (43, 45), (44, 45), (39, 44), None   ),
    ("values",   3, None    , (46, 46), (45, 45), (44, 45)),
    ("attend",   3, (47, 47), None    , (46, 47), None   ),
    ("turn",     3, (47, 49), None    , None    , None   ),
    ("norm",     3, None    , None    , (47, 47), (50, 51)),
    ("apply",    3, None    , None    , (47, 48), None   ),
    ("refill",   0, None    , (48, 49), None    , (48, 51)),
)
SLACK = 1 + max(max(at) for row in LATE for at in row[2:] if at) - STAGE
POWER_SPOTS = (2, 4, 6, 8, 12, 14, 16, 18)
MASK_SPOTS = (9, 10, 13, 15, 17)
LAST_SPOT = 2 * TURNS - 1


def norm_order(engine):
    at = sorted((row[engine][b], i, row[1], b) for i, row in enumerate(LATE) if row[0] == "norm" for b in (0, 1))
    return [(k, b) for _, _, k, b in at]


NORM_TURNS = norm_order(VECTOR)
assert NORM_TURNS == norm_order(POOL)


def norm_count(g, k, b):
    return N_LN * SLOTS * g + len(NORM_TURNS) * (b // 2) + NORM_TURNS.index((k, b % 2)) + 1


def due(engine, at, late, trailing):
    for job, shift in ((trailing, STAGE), (late, 0)):
        if job:
            g, pair = job
            last = isinstance(g, int) and g == GROUPS - 1
            for row in LATE:
                for b in (0, 1):
                    if row[engine] and row[engine][b] == at + shift and not (last and row[0] == "refill"):
                        yield row[0], g, row[1], pair[b]


def spot(at):
    return {1: 2 * (at // PIECES), PIECES - 1: 2 * (at // PIECES) + 1}.get(at % PIECES)


def turns(gated, late):
    for i in range(TURNS):
        now = (gated[0], i, gated[1][i % 2]) if gated else None
        before = (gated[0], i - 1, gated[1][(i - 1) % 2]) if gated and i else None
        if i == 0 and late:
            before = (late[0], TURNS - 1, late[1][1])
        yield i, now, before


def build(nc, x_nodes, x_channels, adj, adj_t, weights, columns, row_in, out):
    with ExitStack() as ctx:
        def sb(name, shape, dt=F32):
            return ctx.enter_context(nc.sbuf_tensor(name, shape, dt))

        def sem(name):
            return ctx.enter_context(nc.semaphore(name))

        def sems(name):
            return [sem(f"{name}{b}") for b in range(SLOTS)]

        ap_hi = [sb(f"adj{k}_hi", [P, NT, N], F32R) for k in (1, 2, 3)]
        ap_lo = [sb(f"adj{k}_lo", [P, NT, N], F32R) for k in (1, 2, 3)]
        w_in = sb("w_in", [P, 19, P])
        w_hi = sb("w_hi", [P, 16, P], F32R)
        w_lo = sb("w_lo", [P, 16, P], F32R)
        cols = sb("cols", [P, 9])
        rows = sb("rows", [1, P + 2])
        wrgb = sb("wrgb", [P, P + 2])
        ident = sb("ident", [P, P])
        ones = sb("ones", [P, P])
        bias_r = sb("bias_r", [P, 1])
        bias_z = sb("bias_z", [P, 1])
        bias_h = sb("bias_h", [P, 1])
        bias_in = sb("bias_in", [P, 2])
        wo_att = sb("wo_att", [P, 3])
        half_neg = sb("half_neg", [P, NT])
        eps = sb("eps", [P, NT])
        low_neg = sb("low_neg", [P, NT, HALF])
        up_mask = sb("up_mask", [P, NT, HALF], F32R)
        no_up = sb("no_up", [P, NT])
        any_up = sb("any_up", [P, NT])
        up_neg = sb("up_neg", [P, NT])
        up_count = sb("up_count", [P, NT])

        x_in = sb("x_in", [P, SLOTS, N])
        h_ch = sb("h_ch", [P, SLOTS, N])
        chan32 = sb("chan32", [P, SLOTS, N])
        nodes32 = sb("nodes32", [P, SLOTS, N])
        work = sb("work", [P, SLOTS, 2 * N])
        row32 = sb("row32", [P, SLOTS, N])
        nodes_hi_t = sb("nodes_hi_t", [P, SLOTS, N], F32R)
        nodes_lo_t = sb("nodes_lo_t", [P, SLOTS, N], F32R)
        agg_hi_t = sb("agg_hi_t", [P, SLOTS, N], F32R)
        agg_lo_t = sb("agg_lo_t", [P, SLOTS, N], F32R)
        chan_hi_t = sb("chan_hi_t", [P, SLOTS, N], F32R)
        chan_lo_t = sb("chan_lo_t", [P, SLOTS, N], F32R)
        rank_hi_t = sb("rank_hi_t", [P, SLOTS, P], F32R)
        rank_lo_t = sb("rank_lo_t", [P, SLOTS, P], F32R)
        stats_t = sb("stats_t", [P, SLOTS, NT, 6])
        moments_t = sb("moments_t", [P, SLOTS, NT, 2])
        var_t = sb("var_t", [P, SLOTS, NT])
        rstd_t = sb("rstd_t", [P, SLOTS, NT])
        xsum_t = sb("xsum_t", [P, SLOTS, 1])
        tcol_t = sb("tcol_t", [P, SLOTS, 1])
        mix_t = sb("mix_t", [P, SLOTS, 1])
        ccol_t = sb("ccol_t", [P, SLOTS, 1])
        spread_t = sb("spread_t", [P, SLOTS, P])
        trash = sb("trash", [P, N])
        pair_t = sb("pair_t", [P, SLOTS, 2])
        pairl_t = sb("pairl_t", [P, SLOTS, 2])
        lmax_t = sb("lmax_t", [P, SLOTS, NT])
        umax_t = sb("umax_t", [P, SLOTS, NT])
        nmax_t = sb("nmax_t", [P, SLOTS, NT])
        udif_t = sb("udif_t", [P, SLOTS, NT])
        lsum_t = sb("lsum_t", [P, SLOTS, NT])
        uexp_t = sb("uexp_t", [P, SLOTS, NT])
        usum_t = sb("usum_t", [P, SLOTS, NT])
        den_t = sb("den_t", [P, SLOTS, NT])
        rden_t = sb("rden_t", [P, SLOTS, NT])
        uden_t = sb("uden_t", [P, SLOTS, NT])

        bank_a = [ctx.enter_context(nc.psum_tensor(f"bank_a{b}", [P, N], F32)) for b in range(SLOTS)]
        bank_b = [ctx.enter_context(nc.psum_tensor(f"bank_b{b}", [P, N], F32)) for b in range(SLOTS)]

        adj_loaded, adjt_loaded, w_loaded, cols_loaded, rows_loaded = (
            sem(n) for n in ("adj_loaded", "adjt_loaded", "w_loaded", "cols_loaded", "rows_loaded"))
        adjt_hi, adjt_lo, adjn_hi, adjn_lo = (sem(n) for n in ("adjt_hi", "adjt_lo", "adjn_hi", "adjn_lo"))
        consts_set, bias_sum, w_mixed, w_split, masks_set = (
            sem(n) for n in ("consts_set", "bias_sum", "w_mixed", "w_split", "masks_set"))
        prep_small, prep_small_read, power_ready, power_hi, power_lo = (
            sem(n) for n in ("prep_small", "prep_small_read", "power_ready", "power_hi", "power_lo"))
        loaded, stored = sems("loaded"), sems("stored")
        agg_ready, agg_hi, agg_lo = sems("agg_ready"), sems("agg_hi"), sems("agg_lo")
        h_done = sems("h_done")
        h_hi, h_lo = ([sem(f"{name}{p}") for p in range(len(PAIRS))] for name in ("h_hi", "h_lo"))
        nodes_ready, nodes_hi, nodes_lo = sems("nodes_ready"), sems("nodes_hi"), sems("nodes_lo")
        normed = sems("normed")
        chan_ready, chan_done, chan_hi, chan_lo = (
            sems(n) for n in ("chan_ready", "chan_done", "chan_hi", "chan_lo"))
        out_ready, resid_done = sems("out_ready"), sems("resid_done")
        rgate_ready, r_done, rh_done = sem("rgate_ready"), sem("r_done"), sem("rh_done")
        rh_hi, rh_lo = sem("rh_hi"), sem("rh_lo")
        zgate_ready, z_done = sem("zgate_ready"), sem("z_done")
        cand_ready, cand_done = sem("cand_ready"), sem("cand_done")
        delta_done, gated_done = sem("delta_done"), sem("gated_done")
        moments_done, var_done, rstd_done = (
            sem(n) for n in ("moments_done", "var_done", "rstd_done"))
        first_sum = sem("first_sum")
        sj_ready, t_done, mix_done = sem("sj_ready"), sem("t_done"), sem("mix_done")
        cols_ready, spread_done, ccol_done = sem("cols_ready"), sem("spread_done"), sem("ccol_done")
        rank_hi, rank_lo = sem("rank_hi"), sem("rank_lo")
        vrow_ready, vleak_done, vrow_done = sem("vrow_ready"), sem("vleak_done"), sem("vrow_done")
        pair_ready, pair_done, pairl_done = sem("pair_ready"), sem("pair_done"), sem("pairl_done")
        lmax_done, umax_done, lmax2_done, nmax_done, udif_done = (
            sem(n) for n in ("lmax_done", "umax_done", "lmax2_done", "nmax_done", "udif_done"))
        low_done, up_done, usum_done, den_done, rden_done, uden_done = (
            sem(n) for n in ("low_done", "up_done", "usum_done", "den_done", "rden_done", "uden_done"))
        att_ready, hlow_done, hup_done, hup_hi, hup_lo = (
            sem(n) for n in ("att_ready", "hlow_done", "hup_done", "hup_hi", "hup_lo"))

        rh_hi_t, rh_lo_t = nodes_hi_t, nodes_lo_t

        adj32 = work[:, 0:2, :].rearrange("p s (t n) -> p (s t) n", t=2)
        adjn_high = (chan_hi_t[:, 2:4, :], agg_hi_t[:, 2:4, :])
        adjn_low = (chan_lo_t[:, 2:4, :], agg_lo_t[:, 2:4, :])
        mixed = work[:, 2:4, :].rearrange("p s (w o) -> p (s w) o", o=P)
        adjt32 = row32
        up32 = work[:, 3, :].rearrange("p (t n) -> p t n", t=NT)
        power_bank = [bank_a[2], bank_b[2], bank_a[3], bank_b[3]]

        block = ctx.enter_context(nc.Block())

        @block.sync
        def _(sp):
            for b in range(SLOTS):
                sp.sem_inc(normed[b], PRIMED)
                sp.sem_inc(stored[b], PRIMED)

            def load(g, b):
                sp.dma_start(x_in[:, b, :].rearrange("p (t c) -> p t c", t=NT),
                             x_nodes[g * SLOTS + b].rearrange("(t p) c -> p t c", p=P)).then_inc(loaded[b], 16)
                sp.dma_start(h_ch[:, b, :], x_channels[g * SLOTS + b]).then_inc(loaded[b], 16)

            def reload(g, b):
                sp.wait_ge(first_sum, SLOTS * g + b + 1)
                sp.wait_ge(nodes_ready[b], N_NODES * g + STEPS)
                load(g + 1, b)

            def store(g, b):
                sp.wait_ge(normed[b], N_LN * g + N_LN + PRIMED)
                sp.dma_start(out[g * SLOTS + b].rearrange("(t p) c -> p t c", p=P),
                             nodes32[:, b, :].rearrange("p (t c) -> p t c", t=NT)).then_inc(stored[b], 16)

            sp.dma_start(adjt32[:, :, :], adj_t.rearrange("(t p) n -> p t n", p=P)).then_inc(adjt_loaded, 16)
            load(0, 0)
            load(0, 1)
            sp.dma_start(adj32, adj.rearrange("(t p) n -> p t n", p=P)).then_inc(adj_loaded, 16)
            load(0, 2)
            load(0, 3)
            with sp.Fori(0, GROUPS - 1) as g:
                for pair in PAIRS:
                    for b in pair:
                        reload(g, b)
                    for b in pair:
                        store(g, b)
            for b in range(SLOTS):
                store(GROUPS - 1, b)
            for b in range(SLOTS):
                sp.wait_ge(stored[b], 16 * GROUPS + PRIMED)

        @block.gpsimd
        def _(pool):
            pool.memset(half_neg[:, :], -0.5).then_inc(consts_set, 1)
            pool.memset(ones[:, :], 1.0).then_inc(consts_set, 1)
            pool.memset(ident[:, :], 0.0).then_inc(consts_set, 1)
            pool.memset(eps[:, :], EPS).then_inc(consts_set, 1)
            pool.wait_ge(consts_set, 4)
            pool.affine_select(out=ident[:, :], in_=ident[:, :], compare_op=ALU.not_equal, fill=1.0,
                               base=0, pattern=[[-1, P]], channel_multiplier=1).then_inc(consts_set, 1)

            def low_part(low, full, high, ready, n, done):
                pool.wait_ge(ready, n)
                pool.tensor_tensor(low, full, high.bitcast(F32), ALU.subtract).then_inc(done, 1)

            def fill(g, b):
                low_part(nodes_lo_t[:, b, :], x_in[:, b, :], nodes_hi_t[:, b, :],
                         nodes_hi[b], N_SPLIT * g + 1, nodes_lo[b])

            def state_low(g, i, b):
                low_part(chan_lo_t[:, b, :], h_ch[:, b, :], chan_hi_t[:, b, :],
                         h_hi[b // 2], state_count(g, i), h_lo[b // 2])

            def late_phase(phase, g, k, b):
                if phase == "norm":
                    n = norm_count(g, k, b)
                    pool.wait_ge(var_done, n)
                    pool.tensor_tensor(rstd_t[:, b, :], var_t[:, b, :], half_neg[:, :], ALU.pow).then_inc(rstd_done, 1)
                elif phase == "apply":
                    low_part(nodes_lo_t[:, b, :], nodes32[:, b, :], nodes_hi_t[:, b, :],
                             nodes_hi[b], N_SPLIT * g + STEPS + k + 1, nodes_lo[b])
                elif phase == "channels":
                    pool.wait_ge(chan_hi[b], N_CHAN * g + k + 1)
                    low_part(chan_lo_t[:, b, :], chan32[:, b, :], chan_hi_t[:, b, :],
                             chan_done[b], N_CHAN * g + k + 1, chan_lo[b])
                elif phase == "values":
                    low_part(nodes_lo_t[:, b, :], row32[:, b, :], nodes_hi_t[:, b, :],
                             hup_hi, SLOTS * g + b + 1, hup_lo)
                elif phase == "refill":
                    fill(g + 1, b)
                    state_low(g + 1, b % 2, b)

            def turn_state(g, i, b):
                if i // 2 < STEPS - 1:
                    state_low(g, i + 2, b)

            def reset_state(g, i, b):
                low_part(rh_lo_t[:, b, :], work[:, b, 0:N], rh_hi_t[:, b, :], rh_hi, gated_count(g, i, b), rh_lo)

            def late_phases(at, late, trailing):
                for phase, g, k, b in due(POOL, at, late, trailing):
                    late_phase(phase, g, k, b)

            def stage(gated, late, trailing):
                for i, now, before in turns(gated, late):
                    for piece in range(PIECES):
                        if before and piece == 3:
                            turn_state(*before)
                        if now and piece == 4:
                            reset_state(*now)
                        late_phases(PIECES * i + piece, late, trailing)

            def finish(trailing):
                for at in range(SLACK):
                    late_phases(at, None, trailing)

            for b in PAIRS[0]:
                fill(0, b)
                state_low(0, b % 2, b)
            for b in PAIRS[1]:
                fill(0, b)
            first, second = PAIRS
            stage((0, first), None, None)
            for b in second:
                state_low(0, b % 2, b)
            stage((0, second), (0, first), None)
            with pool.Fori(0, GROUPS - 2) as g:
                stage((g + 1, first), (g, second), (g, first))
                stage((g + 1, second), (g + 1, first), (g, second))
            stage((GROUPS - 1, first), (GROUPS - 2, second), (GROUPS - 2, first))
            stage((GROUPS - 1, second), (GROUPS - 1, first), (GROUPS - 2, second))
            stage(None, (GROUPS - 1, second), (GROUPS - 1, first))
            finish((GROUPS - 1, second))

        @block.scalar
        def _(act):
            act.dma_start(w_in[:, :, :], weights).then_inc(w_loaded, 16)
            act.dma_start(cols[:, :], columns).then_inc(cols_loaded, 16)
            act.dma_start(rows[:, :], row_in).then_inc(rows_loaded, 16)
            act.wait_ge(adjt_loaded, 16)
            for t in range(NT):
                act.activation(ap_hi[0][:, t, :], adjt32[:, t, :], ACT.Copy).then_inc(adjt_hi, 1)

            def fill(g, b):
                act.wait_ge(loaded[b], 32 * g + 32)
                act.activation(nodes_hi_t[:, b, :], x_in[:, b, :], ACT.Copy).then_inc(nodes_hi[b], 1)

            def state_high(b):
                act.activation(chan_hi_t[:, b, :], h_ch[:, b, :], ACT.Copy).then_inc(h_hi[b // 2], 1)

            for b in PAIRS[0]:
                fill(0, b)
                state_high(b)

            def weights_high(n):
                part = W_PARTS[n]
                act.wait_ge(w_mixed, n + 1)
                act.activation(w_hi[:, part, :], mixed[:, part, :], ACT.Copy).then_inc(w_split, 1)

            weights_high(0)
            act.wait_ge(adj_loaded, 16)
            for n, high in enumerate(adjn_high):
                act.activation(high, adj32[:, 2 * n:2 * n + 2, :], ACT.Copy).then_inc(adjn_hi, 1)

            def prepare(n):
                if n == 0:
                    weights_high(1)
                elif n == 1:
                    fill(0, 2)
                    fill(0, 3)
                elif n in POWER_SPOTS:
                    k, t = divmod(POWER_SPOTS.index(n), NT)
                    act.wait_ge(power_ready, NT * k + t + 1)
                    act.activation(ap_hi[k + 1][:, t, :], power_bank[t][:, :], ACT.Copy).then_inc(power_hi, 1)

            def neighbours(g, i, b):
                act.wait_ge(agg_ready[b], N_AGG * g + i // 2 + 1)
                act.activation(agg_hi_t[:, b, :], bank_a[b][:, :], ACT.Copy).then_inc(agg_hi[b], 1)

            def candidate(g, i, b):
                act.wait_ge(cand_ready, gated_count(g, i, b))
                act.activation(work[:, b, N:2 * N], bank_a[b][:, :], ACT.Tanh,
                               bias=bias_h[:, :]).then_inc(cand_done, 1)

            def reset_gate(g, i, b):
                act.wait_ge(rgate_ready, gated_count(g, i, b))
                act.wait_ge(stored[b], 16 * g + PRIMED)
                act.activation(nodes32[:, b, :], bank_b[b][:, :], ACT.Tanh,
                               bias=bias_r[:, :], scale=0.5).then_inc(r_done, 1)

            def turn_state(g, i, b):
                if i // 2 < STEPS - 1:
                    act.wait_ge(nodes_ready[b], N_NODES * g + i // 2 + 1)
                    act.activation(nodes_hi_t[:, b, :], bank_b[b][:, :], ACT.Copy).then_inc(nodes_hi[b], 1)
                    act.wait_ge(h_done[b], STEPS * g + i // 2 + 1)
                    state_high(b)

            def reset_state(g, i, b):
                act.wait_ge(rh_done, gated_count(g, i, b))
                act.activation(rh_hi_t[:, b, :], work[:, b, 0:N], ACT.Copy).then_inc(rh_hi, 1)

            def update_gate(g, i, b):
                act.wait_ge(zgate_ready, gated_count(g, i, b))
                act.activation(chan32[:, b, :], bank_b[b][:, :], ACT.Tanh,
                               bias=bias_z[:, :], scale=0.5).then_inc(z_done, 1)

            def late_agg(b, n):
                act.wait_ge(agg_ready[b], n)
                act.activation(agg_hi_t[:, b, :], bank_b[b][:, :], ACT.Copy).then_inc(agg_hi[b], 1)

            def late_phase(phase, g, k, b):
                n = SLOTS * g + b + 1
                if phase == "apply":
                    act.wait_ge(normed[b], N_LN * g + k + 1 + PRIMED)
                    act.activation(nodes_hi_t[:, b, :], nodes32[:, b, :], ACT.Copy).then_inc(nodes_hi[b], 1)
                elif phase == "channels":
                    act.wait_ge(chan_ready[b], N_CHAN * g + k + 1)
                    act.activation(chan32[:, b, :], bank_a[b][:, :], ACT.Copy,
                                   accum_out=xsum_t[:, b, :]).then_inc(chan_done[b], 1)
                    act.activation(chan_hi_t[:, b, :], bank_a[b][:, :], ACT.Copy).then_inc(chan_hi[b], 1)
                elif phase == "agg":
                    late_agg(b, N_AGG * g + STEPS + k)
                elif phase == "power" and k < 3:
                    late_agg(b, N_AGG * g + STEPS + 2 + k)
                elif phase == "cols":
                    act.wait_ge(cols_ready, n)
                    act.activation(rank_hi_t[:, b, :], bank_b[b][:, 0:P], ACT.Copy).then_inc(rank_hi, 1)
                elif phase == "rows":
                    act.wait_ge(vrow_ready, n)
                    act.activation(row32[:, b, :], bank_b[b][:, :], ACT.Copy, scale=LEAK).then_inc(vleak_done, 1)
                elif phase == "weights":
                    act.wait_ge(nmax_done, n)
                    for t in range(NT):
                        e = work[:, b, t * HALF:(t + 1) * HALF]
                        ins = act.activation(e, e, ACT.Exp, bias=nmax_t[:, b, t:t + 1],
                                             accum_out=lsum_t[:, b, t:t + 1])
                    ins.then_inc(low_done, 1)
                    act.wait_ge(udif_done, n)
                    act.activation(uexp_t[:, b, :], udif_t[:, b, :], ACT.Exp).then_inc(up_done, 1)
                elif phase == "values":
                    act.wait_ge(hup_done, n)
                    act.activation(nodes_hi_t[:, b, :], row32[:, b, :], ACT.Copy).then_inc(hup_hi, 1)
                elif phase == "refill":
                    act.wait_ge(out_ready[b], N_OUT * g + N_OUT)
                    fill(g + 1, b)
                    state_high(b)

            def late_phases(at, late, trailing, preparing=False):
                if preparing:
                    prepare(spot(at))
                for phase, g, k, b in due(SCALAR, at, late, trailing):
                    late_phase(phase, g, k, b)

            def stage(gated, late, trailing, preparing=False):
                for i, now, before in turns(gated, late):
                    if now:
                        neighbours(*now)
                    late_phases(PIECES * i, late, trailing, preparing)
                    if before:
                        candidate(*before)
                    late_phases(PIECES * i + 1, late, trailing, preparing)
                    if now:
                        reset_gate(*now)
                    late_phases(PIECES * i + 2, late, trailing, preparing)
                    if before:
                        turn_state(*before)
                    late_phases(PIECES * i + 3, late, trailing, preparing)
                    if now:
                        reset_state(*now)
                        update_gate(*now)
                    late_phases(PIECES * i + 4, late, trailing, preparing)

            def finish(trailing):
                for at in range(SLACK):
                    late_phases(at, None, trailing)

            first, second = PAIRS
            stage((0, first), None, None, preparing=True)
            act.wait_ge(power_ready, 2 * NT)
            for b in second:
                state_high(b)
            stage((0, second), (0, first), None)
            with act.Fori(0, GROUPS - 2) as g:
                stage((g + 1, first), (g, second), (g, first))
                stage((g + 1, second), (g + 1, first), (g, second))
            stage((GROUPS - 1, first), (GROUPS - 2, second), (GROUPS - 2, first))
            stage((GROUPS - 1, second), (GROUPS - 1, first), (GROUPS - 2, second))
            stage(None, (GROUPS - 1, second), (GROUPS - 1, first))
            finish((GROUPS - 1, second))

        @block.vector
        def _(dve):
            for t in range(NT):
                dve.wait_ge(adjt_hi, t + 1)
                dve.tensor_tensor(ap_lo[0][:, t, :], adjt32[:, t, :], ap_hi[0][:, t, :].bitcast(F32),
                                  ALU.subtract).then_inc(adjt_lo, 1)
            dve.wait_ge(w_loaded, 16)
            dve.wait_ge(cols_loaded, 16)
            dve.wait_ge(prep_small, 1)
            dve.wait_ge(consts_set, 5)
            dve.tensor_copy(wrgb[:, :], bank_b[0][:, 0:P + 2]).then_inc(prep_small_read, 1)
            dve.tensor_copy(wo_att[:, 0:2], bank_b[1][:, 0:2]).then_inc(prep_small_read, 1)
            dve.wait_ge(prep_small_read, 2)
            dve.tensor_tensor(wo_att[:, 2:3], wo_att[:, 0:1], wo_att[:, 1:2], ALU.add).then_inc(prep_small_read, 1)
            dve.tensor_tensor(mixed[:, S_R, :], w_in[:, W4A, :], w_in[:, W4B, :], ALU.add).then_inc(prep_small_read, 1)
            dve.tensor_tensor(mixed[:, S_H, :], w_in[:, W5A, :], w_in[:, W5B, :], ALU.add)
            dve.tensor_tensor(mixed[:, S_ZR, :], w_in[:, W3A, :], w_in[:, W3B, :], ALU.add).then_inc(prep_small_read, 1)
            dve.tensor_copy(mixed[:, S_U3, :], w_in[:, U3, :])
            dve.tensor_scalar(mixed[:, S_U5, :], w_in[:, U5, :], 0.5, None, ALU.mult)
            dve.tensor_tensor(bias_in[:, 0:1], cols[:, B4:B4 + 1], cols[:, BU3:BU3 + 1], ALU.add).then_inc(bias_sum, 1)
            dve.tensor_tensor(bias_in[:, 1:2], cols[:, B3:B3 + 1], cols[:, BU3:BU3 + 1], ALU.add).then_inc(bias_sum, 1)
            dve.wait_ge(bias_sum, 2)
            dve.tensor_scalar(bias_r[:, :], bias_in[:, 0:1], 0.5, None, ALU.mult)
            dve.tensor_scalar(bias_z[:, :], bias_in[:, 1:2], 0.5, None, ALU.mult)
            dve.tensor_tensor(bias_h[:, :], cols[:, B5:B5 + 1], cols[:, BU5:BU5 + 1], ALU.add)
            dve.wait_ge(prep_small_read, 5)
            dve.tensor_tensor(mixed[:, S_ZR, :], mixed[:, S_ZR, :], mixed[:, S_R, :], ALU.subtract).then_inc(w_mixed, 1)

            def weights_low(n):
                part = W_PARTS[n]
                dve.wait_ge(w_split, 2 * n + 1)
                dve.tensor_tensor(w_lo[:, part, :], mixed[:, part, :], w_hi[:, part, :].bitcast(F32),
                                  ALU.subtract).then_inc(w_split, 1)

            weights_low(0)
            dve.tensor_scalar(mixed[:, S_W1, :], w_in[:, W1, :], wrgb[:, P:P + 1], None, ALU.mult)
            dve.tensor_copy(mixed[:, S_X0, :], w_in[:, C0, :])
            dve.tensor_tensor(mixed[:, S_X1:S_X3 + 1, :], w_in[:, C1:C3 + 1, :], w_in[:, C4:C6 + 1, :], ALU.add)
            dve.tensor_copy(mixed[:, S_WO:S_WS + 1, :], w_in[:, WO:WS + 1, :])
            dve.tensor_scalar(mixed[:, S_SJ, :], ones[:, :], cols[:, WJ:WJ + 1], None, ALU.mult)
            dve.wait_ge(prep_small_read, 3)
            dve.tensor_scalar(mixed[:, S_V, :], ones[:, :], wo_att[:, 2:3], None, ALU.mult)
            dve.tensor_scalar(mixed[:, S_P1, :], ones[:, :], wo_att[:, 0:1], None, ALU.mult)
            dve.tensor_scalar(mixed[:, S_P2, :], ones[:, :], wo_att[:, 1:2], None, ALU.mult).then_inc(w_mixed, 1)

            def masks(part):
                if part == 0:
                    dve.wait_ge(w_split, 4)
                    dve.tensor_scalar(low_neg[:, :, :], adjt32[:, :, 0:HALF], 0.0, -NEG_BIG, ALU.is_gt, ALU.mult).then_inc(masks_set, 1)
                    dve.tensor_scalar(up32, adjt32[:, :, HALF:N], 0.0, None, ALU.is_gt).then_inc(masks_set, 1)
                elif part == 1:
                    dve.wait_ge(masks_set, 2)
                    dve.tensor_scalar(low_neg[:, :, :], low_neg[:, :, :], NEG_BIG, None, ALU.add).then_inc(masks_set, 1)
                elif part == 2:
                    dve.wait_ge(masks_set, 2)
                    dve.tensor_reduce(any_up[:, :], up32, AX_X, ALU.max).then_inc(masks_set, 1)
                elif part == 3:
                    dve.wait_ge(masks_set, 4)
                    dve.tensor_scalar(no_up[:, :], any_up[:, :], -1.0, 1.0, ALU.mult, ALU.add).then_inc(masks_set, 1)
                    dve.wait_ge(masks_set, 5)
                    dve.tensor_scalar(up_neg[:, :], no_up[:, :], NEG_BIG, None, ALU.mult)
                    for t in range(NT):
                        dve.tensor_scalar(up_mask[:, t, :], up32[:, t, :], no_up[:, t:t + 1], None, ALU.max).then_inc(masks_set, 1)
                else:
                    dve.wait_ge(masks_set, 5 + NT)
                    dve.tensor_reduce(up_count[:, :], up_mask[:, :, :].bitcast(F32), AX_X, ALU.add).then_inc(masks_set, 1)

            def prepare(n):
                if n == 0:
                    dve.wait_ge(adjn_hi, 2)
                    for m, (high, low) in enumerate(zip(adjn_high, adjn_low)):
                        dve.tensor_tensor(low, adj32[:, 2 * m:2 * m + 2, :], high.bitcast(F32),
                                          ALU.subtract).then_inc(adjn_lo, 1)
                    dve.wait_ge(adjn_lo, 2)
                elif n == 1:
                    weights_low(1)
                elif n in POWER_SPOTS:
                    k, t = divmod(POWER_SPOTS.index(n), NT)
                    dve.wait_ge(power_hi, NT * k + t + 1)
                    dve.tensor_tensor(ap_lo[k + 1][:, t, :], power_bank[t][:, :],
                                      ap_hi[k + 1][:, t, :].bitcast(F32), ALU.subtract).then_inc(power_lo, 1)
                elif n in MASK_SPOTS:
                    masks(MASK_SPOTS.index(n))

            def agg_low(b, n, bank):
                dve.wait_ge(agg_hi[b], n)
                dve.tensor_tensor(agg_lo_t[:, b, :], bank[b][:, :], agg_hi_t[:, b, :].bitcast(F32),
                                  ALU.subtract).then_inc(agg_lo[b], 1)

            def neighbours(g, i, b):
                agg_low(b, N_AGG * g + i // 2 + 1, bank_a)

            def reset_gate(g, i, b):
                dve.wait_ge(loaded[b], 32 * g + 32)
                dve.wait_ge(r_done, gated_count(g, i, b))
                dve.scalar_tensor_tensor(out=work[:, b, 0:N], in0=nodes32[:, b, :], scalar=1.0,
                                         in1=h_ch[:, b, :], op0=ALU.add, op1=ALU.mult).then_inc(rh_done, 1)

            def turn_state(g, i, b):
                if i // 2 < STEPS - 1:
                    dve.wait_ge(nodes_hi[b], N_SPLIT * g + i // 2 + 2)
                    dve.tensor_tensor(nodes_lo_t[:, b, :], bank_b[b][:, :], nodes_hi_t[:, b, :].bitcast(F32),
                                      ALU.subtract).then_inc(nodes_lo[b], 1)

            def candidate(g, i, b):
                n = gated_count(g, i, b)
                cand = work[:, b, N:2 * N]
                dve.wait_ge(cand_done, n)
                dve.tensor_tensor(cand, cand, h_ch[:, b, :], ALU.subtract).then_inc(delta_done, 1)
                dve.wait_ge(z_done, n)
                dve.wait_ge(delta_done, n)
                dve.scalar_tensor_tensor(out=cand, in0=chan32[:, b, :], scalar=1.0, in1=cand,
                                         op0=ALU.add, op1=ALU.mult).then_inc(gated_done, 1)
                dve.wait_ge(gated_done, n)
                dve.scalar_tensor_tensor(out=h_ch[:, b, :], in0=cand, scalar=0.5, in1=h_ch[:, b, :],
                                         op0=ALU.mult, op1=ALU.add).then_inc(h_done[b], 1)

            def norm(g, k, b):
                n = N_LN * g + k + 1
                if k == 0:
                    dve.wait_ge(nodes_ready[b], N_NODES * g + STEPS)
                    dve.tensor_tensor(nodes32[:, b, :], bank_b[b][:, :], x_in[:, b, :], ALU.add).then_inc(first_sum, 1)
                    dve.wait_ge(first_sum, SLOTS * g + b + 1)
                    y = nodes32[:, b, :]
                else:
                    dve.wait_ge(nodes_ready[b], N_NODES * g + STEPS + k)
                    y = bank_b[b][:, :]
                for t in range(NT):
                    dve.bn_stats(stats_t[:, b, t, :], y[:, t * P:(t + 1) * P])
                dve.drain()
                for t in range(NT):
                    ins = dve.bn_aggr(moments_t[:, b, t, :], stats_t[:, b, t, :])
                ins.then_inc(moments_done, 1)
                dve.wait_ge(moments_done, norm_count(g, k, b))
                dve.tensor_tensor(var_t[:, b, :], moments_t[:, b, :, 1], eps[:, :], ALU.add).then_inc(var_done, 1)

            def apply_norm(g, k, b):
                y = bank_b[b] if k else nodes32[:, b, :]
                dve.wait_ge(rstd_done, norm_count(g, k, b))
                for t in range(NT):
                    ins = dve.tensor_scalar(nodes32[:, b, t * P:(t + 1) * P], y[:, t * P:(t + 1) * P],
                                            moments_t[:, b, t, 0:1], rstd_t[:, b, t:t + 1],
                                            ALU.subtract, ALU.mult)
                ins.then_inc(normed[b], 1)

            def relation_sums(g, b):
                n = SLOTS * g + b + 1
                dve.wait_ge(chan_done[b], N_CHAN * g + 1)
                dve.tensor_scalar(spread_t[:, b, :], wrgb[:, 0:P], xsum_t[:, b, :], None,
                                  ALU.mult).then_inc(spread_done, 1)
                dve.wait_ge(sj_ready, n)
                dve.wait_ge(chan_done[b], N_CHAN * g + 1)
                dve.tensor_tensor_reduce(trash[:, :], bank_a[b][:, :], chan32[:, b, :], 1.0, 0.0,
                                         ALU.mult, ALU.add, tcol_t[:, b, :]).then_inc(t_done, 1)
                dve.wait_ge(t_done, n)
                dve.scalar_tensor_tensor(out=mix_t[:, b, :], in0=xsum_t[:, b, :], scalar=wrgb[:, P + 1:P + 2],
                                         in1=tcol_t[:, b, :], op0=ALU.mult, op1=ALU.add).then_inc(mix_done, 1)

            def residual(g, k, b, bank, scalar):
                dve.wait_ge(out_ready[b], N_OUT * g + k)
                dve.scalar_tensor_tensor(out=row32[:, b, :], in0=bank[b][:, :], scalar=scalar,
                                         in1=chan32[:, b, :], op0=ALU.add, op1=ALU.add).then_inc(resid_done[b], 1)

            def logits(g, b):
                n = SLOTS * g + b + 1
                dve.wait_ge(vleak_done, n)
                dve.tensor_tensor(row32[:, b, :], bank_b[b][:, :], row32[:, b, :], ALU.max).then_inc(vrow_done, 1)
                dve.wait_ge(pair_ready, n)
                for c in range(2):
                    if c:
                        dve.wait_ge(pair_done, 2 * n - 1)
                    dve.tensor_tensor_reduce(trash[:, 0:P], bank_a[b][:, c * P:(c + 1) * P], ident[:, :], 1.0, 0.0,
                                             ALU.mult, ALU.add, pair_t[:, b, c:c + 1]).then_inc(pair_done, 1)
                dve.wait_ge(pair_done, 2 * n)
                dve.scalar_tensor_tensor(out=pairl_t[:, b, :], in0=pair_t[:, b, :], scalar=LEAK,
                                         in1=pair_t[:, b, :], op0=ALU.mult, op1=ALU.max).then_inc(pairl_done, 1)

            def maxima(g, b):
                n = SLOTS * g + b + 1
                dve.wait_ge(vrow_done, n)
                dve.wait_ge(pairl_done, n)
                for c in range(2):
                    ins = dve.tensor_tensor(umax_t[:, b, 2 * c:2 * c + 2], pairl_t[:, b, :],
                                            up_neg[:, 2 * c:2 * c + 2], ALU.add)
                ins.then_inc(umax_done, 1)
                for t in range(NT):
                    ins = dve.tensor_tensor_reduce(work[:, b, t * HALF:(t + 1) * HALF],
                                                   row32[:, b, t // 2:N:2], low_neg[:, t, :], 1.0, 3 * NEG_BIG,
                                                   ALU.add, ALU.max, lmax_t[:, b, t:t + 1])
                ins.then_inc(lmax_done, 1)
                dve.wait_ge(lmax_done, n)
                dve.wait_ge(umax_done, n)
                dve.tensor_tensor(lmax_t[:, b, :], lmax_t[:, b, :], umax_t[:, b, :], ALU.max).then_inc(lmax2_done, 1)
                dve.wait_ge(lmax2_done, n)
                dve.tensor_scalar(nmax_t[:, b, :], lmax_t[:, b, :], -1.0, None, ALU.mult).then_inc(nmax_done, 1)
                dve.tensor_tensor(udif_t[:, b, :], umax_t[:, b, :], lmax_t[:, b, :], ALU.subtract).then_inc(udif_done, 1)

            def values(g, b):
                n = SLOTS * g + b + 1
                dve.wait_ge(up_done, n)
                dve.tensor_tensor(usum_t[:, b, :], uexp_t[:, b, :], up_count[:, :], ALU.mult).then_inc(usum_done, 1)
                dve.wait_ge(usum_done, n)
                dve.wait_ge(low_done, n)
                dve.tensor_tensor(den_t[:, b, :], usum_t[:, b, :], lsum_t[:, b, :], ALU.add).then_inc(den_done, 1)
                dve.wait_ge(den_done, n)
                dve.reciprocal(rden_t[:, b, :], den_t[:, b, :]).then_inc(rden_done, 1)
                dve.wait_ge(rden_done, n)
                dve.tensor_tensor(uden_t[:, b, :], uexp_t[:, b, :], rden_t[:, b, :], ALU.mult).then_inc(uden_done, 1)
                dve.wait_ge(att_ready, n)
                dve.wait_ge(uden_done, n)
                h = bank_a[b][:, :].rearrange("p (t c) -> p t c", t=NT)
                dve.tensor_tensor(row32[:, b, :].rearrange("p (t c) -> p t c", t=NT), h,
                                  uden_t[:, b, :].unsqueeze(2).to_broadcast([P, NT, P]), ALU.mult).then_inc(hup_done, 1)
                dve.tensor_tensor(nodes32[:, b, :].rearrange("p (t c) -> p t c", t=NT), h,
                                  rden_t[:, b, :].unsqueeze(2).to_broadcast([P, NT, P]), ALU.mult).then_inc(hlow_done, 1)

            def late_phase(phase, g, k, b):
                n = SLOTS * g + b + 1
                if phase == "norm":
                    norm(g, k, b)
                elif phase == "apply":
                    apply_norm(g, k, b)
                elif phase == "agg":
                    agg_low(b, N_AGG * g + STEPS + k, bank_b)
                elif phase == "power" and k < 3:
                    agg_low(b, N_AGG * g + STEPS + 2 + k, bank_b)
                elif phase == "power":
                    residual(g, 2, b, bank_a, 0.0)
                elif phase == "sj":
                    relation_sums(g, b)
                elif phase == "cols":
                    dve.wait_ge(rank_hi, n)
                    dve.tensor_tensor(rank_lo_t[:, b, :], bank_b[b][:, 0:P],
                                      rank_hi_t[:, b, :].bitcast(F32), ALU.subtract).then_inc(rank_lo, 1)
                    dve.tensor_tensor(ccol_t[:, b, :], bank_b[b][:, P:P + 1], cols[:, BIAS1:BIAS1 + 1],
                                      ALU.add).then_inc(ccol_done, 1)
                elif phase == "out1":
                    dve.wait_ge(ccol_done, n)
                    residual(g, 1, b, bank_a, ccol_t[:, b, :])
                elif phase == "rows":
                    logits(g, b)
                elif phase == "weights":
                    maxima(g, b)
                elif phase == "values":
                    values(g, b)
                elif phase == "attend":
                    residual(g, 3, b, bank_b, 0.0)

            def late_phases(at, late, trailing, preparing=False):
                if preparing:
                    prepare(spot(at))
                for phase, g, k, b in due(VECTOR, at, late, trailing):
                    late_phase(phase, g, k, b)

            def stage(gated, late, trailing, preparing=False):
                for i, now, before in turns(gated, late):
                    if now:
                        neighbours(*now)
                    late_phases(PIECES * i, late, trailing, preparing)
                    if before:
                        candidate(*before)
                    late_phases(PIECES * i + 1, late, trailing, preparing)
                    if now:
                        reset_gate(*now)
                    late_phases(PIECES * i + 2, late, trailing, preparing)
                    if before:
                        turn_state(*before)
                    late_phases(PIECES * i + 3, late, trailing, preparing)
                    late_phases(PIECES * i + 4, late, trailing, preparing)

            def finish(trailing):
                for at in range(SLACK):
                    late_phases(at, None, trailing)

            first, second = PAIRS
            stage((0, first), None, None, preparing=True)
            stage((0, second), (0, first), None)
            with dve.Fori(0, GROUPS - 2) as g:
                stage((g + 1, first), (g, second), (g, first))
                stage((g + 1, second), (g + 1, first), (g, second))
            stage((GROUPS - 1, first), (GROUPS - 2, second), (GROUPS - 2, first))
            stage((GROUPS - 1, second), (GROUPS - 1, first), (GROUPS - 2, second))
            stage(None, (GROUPS - 1, second), (GROUPS - 1, first))
            finish((GROUPS - 1, second))

        @block.tensor
        def _(pe):
            def split_product(psum, lhs, rhs, start, stop, low_ready=None, low_count=None):
                pe.matmul(psum, lhs[0], rhs[0], start=start, stop=False)
                pe.matmul(psum, lhs[1], rhs[0], start=False, stop=False)
                if low_ready is not None:
                    pe.wait_ge(low_ready, low_count)
                return pe.matmul(psum, lhs[0], rhs[1], start=False, stop=stop)

            def weight(n):
                return w_hi[:, n, :], w_lo[:, n, :]

            def tile_of(hi, lo, b, t):
                return hi[:, b, t * P:(t + 1) * P], lo[:, b, t * P:(t + 1) * P]

            def neighbour_sum(b, k, psum, n=None):
                if n is not None:
                    pe.wait_ge(nodes_hi[b], n)
                for t in range(NT):
                    hi = nodes_hi_t[:, b, t * P:(t + 1) * P]
                    pe.matmul(psum, hi, ap_hi[k - 1][:, t, :], start=(t == 0), stop=False)
                    pe.matmul(psum, hi, ap_lo[k - 1][:, t, :], start=False, stop=False)
                if n is not None:
                    pe.wait_ge(nodes_lo[b], n)
                for t in range(NT):
                    ins = pe.matmul(psum, nodes_lo_t[:, b, t * P:(t + 1) * P], ap_hi[k - 1][:, t, :],
                                    start=False, stop=(t == NT - 1))
                ins.then_inc(agg_ready[b], 1)

            def turn(psum, source):
                for t in range(NT):
                    ins = pe.transpose(psum[:, t * P:(t + 1) * P], source[:, t * P:(t + 1) * P], ident[:, :])
                return ins

            pe.wait_ge(consts_set, 5)
            pe.wait_ge(rows_loaded, 16)
            pe.matmul(bank_b[0][:, 0:P + 2], ones[0:1, :], rows[:, :], start=True, stop=True)
            pe.wait_ge(w_loaded, 16)
            pe.wait_ge(cols_loaded, 16)
            pe.matmul(bank_b[1][:, 0:2], w_in[:, WOT, :], cols[:, A1:A2 + 1], start=True, stop=True).then_inc(prep_small, 1)

            def prepare(n):
                if n in POWER_SPOTS:
                    k, m = divmod(POWER_SPOTS.index(n), NT)
                    if m == 0:
                        if k == 0:
                            pe.wait_ge(adjn_lo, 2)
                        else:
                            pe.wait_ge(power_lo, NT)
                    for t in range(NT):
                        high, low = adjn_high[t // 2], adjn_low[t // 2]
                        ins = split_product(power_bank[m][:, :], tile_of(high, low, t % 2, m),
                                            (ap_hi[k][:, t, :], ap_lo[k][:, t, :]), t == 0, t == NT - 1)
                    ins.then_inc(power_ready, 1)
                elif n == LAST_SPOT:
                    pe.wait_ge(power_lo, 2 * NT)
                    pe.wait_ge(masks_set, 6 + NT)
                    pe.wait_ge(w_split, 4)

            def neighbours(g, i, b):
                neighbour_sum(b, 1, bank_a[b][:, :], N_SPLIT * g + i // 2 + 1)

            def candidate(g, i, b):
                n = gated_count(g, i, b)
                u_hi, u_lo = weight(S_U5)
                pe.wait_ge(rh_hi, n)
                pe.matmul(bank_a[b][:, :], u_hi, rh_hi_t[:, b, :], start=False, stop=False)
                pe.matmul(bank_a[b][:, :], u_lo, rh_hi_t[:, b, :], start=False, stop=False)
                pe.wait_ge(rh_lo, n)
                pe.matmul(bank_a[b][:, :], u_hi, rh_lo_t[:, b, :], start=False, stop=True).then_inc(cand_ready, 1)

            def reset_gate(g, i, b):
                pe.wait_ge(normed[b], N_LN * g + PRIMED)
                pe.wait_ge(h_hi[b // 2], state_count(g, i))
                split_product(bank_b[b][:, :], weight(S_U3), (chan_hi_t[:, b, :], chan_lo_t[:, b, :]), True, False,
                              h_lo[b // 2], state_count(g, i))
                agg = (agg_hi_t[:, b, :], agg_lo_t[:, b, :])
                n = N_AGG * g + i // 2 + 1
                pe.wait_ge(agg_hi[b], n)
                split_product(bank_b[b][:, :], weight(S_R), agg, False, True, agg_lo[b], n).then_inc(rgate_ready, 1)
                split_product(bank_a[b][:, :], weight(S_H), agg, True, False)

            def turn_state(g, i, b):
                pe.wait_ge(h_done[b], STEPS * g + i // 2 + 1)
                turn(bank_b[b], h_ch[:, b, :]).then_inc(nodes_ready[b], 1)

            def update_gate(g, i, b):
                pe.wait_ge(r_done, gated_count(g, i, b))
                for w, a, last in ((w_hi, agg_hi_t, False), (w_hi, agg_lo_t, False), (w_lo, agg_hi_t, True)):
                    ins = pe.matmul(bank_b[b][:, :], w[:, S_ZR, :], a[:, b, :], start=False, stop=last,
                                    skip_group_check=True)
                ins.then_inc(zgate_ready, 1)

            def power(g, k, b):
                n = N_AGG * g + STEPS + 1 + k
                if k == 1:
                    pe.wait_ge(chan_lo[b], N_CHAN * g + 2)
                    pe.wait_ge(chan_done[b], N_CHAN * g + 2)
                    split_product(bank_a[b][:, :], weight(S_X0), (chan_hi_t[:, b, :], chan_lo_t[:, b, :]), True, False)
                pe.wait_ge(agg_hi[b], n)
                ins = split_product(bank_a[b][:, :], weight(S_X0 + k), (agg_hi_t[:, b, :], agg_lo_t[:, b, :]), False, k == 3,
                                    agg_lo[b], n)
                if k == 3:
                    ins.then_inc(out_ready[b], 1)
                else:
                    neighbour_sum(b, k + 1, bank_b[b][:, :])

            def att_rows(g, b):
                x = (chan_hi_t[:, b, :], chan_lo_t[:, b, :])
                even = tuple(v[:, 0:N:2] for v in x)
                odd = tuple(v[:, 1:N:2] for v in x)
                pe.wait_ge(chan_hi[b], N_CHAN * g + 3)
                split_product(bank_b[b][:, :], weight(S_V), x, True, True,
                              chan_lo[b], N_CHAN * g + 3).then_inc(vrow_ready, 1)
                split_product(bank_a[b][:, 0:HALF], weight(S_P1), even, True, False)
                split_product(bank_a[b][:, 0:HALF], weight(S_P2), odd, False, True).then_inc(pair_ready, 1)

            def att_values(g, b):
                pe.wait_ge(pair_done, 2 * (SLOTS * g + b + 1))
                for t in range(NT):
                    ins = split_product(bank_a[b][:, t * P:(t + 1) * P], tile_of(chan_hi_t, chan_lo_t, b, t),
                                        weight(S_WO), True, True)
                ins.then_inc(att_ready, 1)
                pe.wait_ge(vrow_done, SLOTS * g + b + 1)
                split_product(bank_b[b][:, :], weight(S_WS), (chan_hi_t[:, b, :], chan_lo_t[:, b, :]), True, False)

            def attend(g, b):
                n = SLOTS * g + b + 1
                pe.wait_ge(hlow_done, n)
                for t in range(NT):
                    pe.matmul(bank_b[b][:, 0:HALF], nodes32[:, b, t * P:(t + 1) * P],
                              work[:, b, t * HALF:(t + 1) * HALF], start=False, stop=False)
                for ready, part in ((hup_hi, nodes_hi_t), (hup_lo, nodes_lo_t)):
                    pe.wait_ge(ready, n)
                    for t in range(NT):
                        ins = pe.matmul(bank_b[b][:, HALF:N], part[:, b, t * P:(t + 1) * P], up_mask[:, t, :],
                                        start=False, stop=(ready is hup_lo and t == NT - 1))
                ins.then_inc(out_ready[b], 1)

            def late_phase(phase, g, k, b):
                n = SLOTS * g + b + 1
                if phase == "channels":
                    pe.wait_ge(normed[b], N_LN * g + k + 1 + PRIMED)
                    turn(bank_a[b], nodes32[:, b, :]).then_inc(chan_ready[b], 1)
                elif phase == "turn":
                    pe.wait_ge(resid_done[b], N_OUT * g + k)
                    turn(bank_b[b], row32[:, b, :]).then_inc(nodes_ready[b], 1)
                elif phase == "agg":
                    neighbour_sum(b, 1, bank_b[b][:, :], N_SPLIT * g + STEPS + k)
                elif phase == "sj":
                    pe.wait_ge(chan_hi[b], N_CHAN * g + 1)
                    split_product(bank_a[b][:, :], weight(S_SJ), (chan_hi_t[:, b, :], chan_lo_t[:, b, :]),
                                  True, True, chan_lo[b], N_CHAN * g + 1).then_inc(sj_ready, 1)
                elif phase == "cols":
                    pe.wait_ge(agg_lo[b], N_AGG * g + STEPS + 1)
                    pe.wait_ge(mix_done, n)
                    pe.wait_ge(spread_done, n)
                    pe.matmul(bank_b[b][:, 0:P], spread_t[:, b, :], w_in[:, W1, :], start=True, stop=True)
                    pe.matmul(bank_b[b][:, P:P + 1], w_in[:, W1, :], mix_t[:, b, :], start=True,
                              stop=True).then_inc(cols_ready, 1)
                elif phase == "out1":
                    split_product(bank_a[b][:, :], weight(S_W1), (agg_hi_t[:, b, :], agg_lo_t[:, b, :]), True, False)
                    pe.wait_ge(rank_hi, n)
                    pe.matmul(bank_a[b][:, :], rank_hi_t[:, b, :], chan_hi_t[:, b, :], start=False, stop=False)
                    pe.matmul(bank_a[b][:, :], rank_hi_t[:, b, :], chan_lo_t[:, b, :], start=False, stop=False)
                    pe.wait_ge(rank_lo, n)
                    pe.matmul(bank_a[b][:, :], rank_lo_t[:, b, :], chan_hi_t[:, b, :], start=False,
                              stop=True).then_inc(out_ready[b], 1)
                elif phase == "power":
                    power(g, k, b)
                elif phase == "rows":
                    att_rows(g, b)
                elif phase == "weights":
                    att_values(g, b)
                elif phase == "attend":
                    attend(g, b)

            def late_phases(at, late, trailing, preparing=False):
                if preparing:
                    prepare(spot(at))
                for phase, g, k, b in due(PE, at, late, trailing):
                    late_phase(phase, g, k, b)

            def stage(gated, late, trailing, preparing=False):
                for i, now, before in turns(gated, late):
                    if now:
                        neighbours(*now)
                    late_phases(PIECES * i, late, trailing, preparing)
                    if before:
                        candidate(*before)
                    late_phases(PIECES * i + 1, late, trailing, preparing)
                    if now:
                        if preparing and i == 0:
                            pe.wait_ge(w_split, 2)
                        reset_gate(*now)
                    late_phases(PIECES * i + 2, late, trailing, preparing)
                    if before:
                        turn_state(*before)
                    late_phases(PIECES * i + 3, late, trailing, preparing)
                    if now:
                        update_gate(*now)
                    late_phases(PIECES * i + 4, late, trailing, preparing)

            def finish(trailing):
                for at in range(SLACK):
                    late_phases(at, None, trailing)

            pe.wait_ge(adjt_lo, NT)
            first, second = PAIRS
            stage((0, first), None, None, preparing=True)
            stage((0, second), (0, first), None)
            with pe.Fori(0, GROUPS - 2) as g:
                stage((g + 1, first), (g, second), (g, first))
                stage((g + 1, second), (g + 1, first), (g, second))
            stage((GROUPS - 1, first), (GROUPS - 2, second), (GROUPS - 2, first))
            stage((GROUPS - 1, second), (GROUPS - 1, first), (GROUPS - 2, second))
            stage(None, (GROUPS - 1, second), (GROUPS - 1, first))
            finish((GROUPS - 1, second))


def kernel(x, adj, L0_gnn_w3_w, L0_gnn_w3_b, L0_gnn_u3_w, L0_gnn_u3_b, L0_gnn_w4_w, L0_gnn_w4_b, L0_gnn_w5_w,
           L0_gnn_w5_b, L0_gnn_u5_w, L0_gnn_u5_b, L1_gnn_g_w, L1_gnn_g_b, L1_gnn_weight, L1_gnn_bias,
           L2_gnn_weight_1, L3_gnn_others_weight, L3_gnn_self_weight, L3_gnn_att_weight):
    import numpy as np
    import concourse.bacc as bacc
    from concourse.bass_utils import run_bass_kernel_spmd

    def halves(w):
        w = np.asarray(w)
        return [w[:, :P].T, w[:, P:].T]

    stacked = [*halves(L0_gnn_w3_w), *halves(L0_gnn_w4_w), *halves(L0_gnn_w5_w),
               np.asarray(L0_gnn_u3_w).T, np.asarray(L0_gnn_u5_w).T, np.asarray(L1_gnn_weight),
               *[np.asarray(L2_gnn_weight_1)[:, :, k] for k in range(7)],
               np.asarray(L3_gnn_others_weight), np.asarray(L3_gnn_self_weight), np.asarray(L3_gnn_others_weight).T]
    g_w = np.asarray(L1_gnn_g_w)
    att = np.asarray(L3_gnn_att_weight)[:, 0]
    columns = [np.asarray(v) for v in (L0_gnn_w3_b, L0_gnn_w4_b, L0_gnn_w5_b, L0_gnn_u3_b, L0_gnn_u5_b)]
    columns += [g_w[:P], np.asarray(L1_gnn_bias), att[:P], att[P:]]
    row = np.concatenate([g_w[P:], np.asarray(L1_gnn_g_b).reshape(1)])[None, :]
    arrays = {
        "x_nodes": np.ascontiguousarray(x),
        "x_channels": np.ascontiguousarray(np.asarray(x).transpose(0, 2, 1)),
        "adj": np.ascontiguousarray(adj),
        "adj_t": np.ascontiguousarray(np.asarray(adj).T),
        "weights": np.ascontiguousarray(np.stack(stacked, axis=1)),
        "columns": np.ascontiguousarray(np.stack(columns, axis=1)),
        "row_in": np.ascontiguousarray(row),
    }
    nc = bacc.Bacc("TRN2", target_bir_lowering=False, num_devices=1)
    args = [nc.dram_tensor(name, a.shape, mybir.dt.from_np(a.dtype), kind="ExternalInput").ap()
            for name, a in arrays.items()]
    out = nc.dram_tensor("out", (BATCH, N, P), F32, kind="ExternalOutput").ap()
    build(nc, *args, out)
    result = run_bass_kernel_spmd(nc, [arrays], core_ids=[0])
    return result.results[0]["out"]
```
